# Optimizing a Trainium2 kernel written in Bass

```python
import numpy as np
import jax
import jax.numpy as jnp

def _softmax(x, axis=-1):
    return jax.nn.softmax(x, axis=axis)

def _gelu(x):
    return jax.nn.gelu(x, approximate=True)

def _silu(x):
    return jax.nn.silu(x)

def _sigmoid(x):
    return jax.nn.sigmoid(x)

def _layernorm(x, axis=-1, eps=1e-05):
    m = jnp.mean(x, axis=axis, keepdims=True)
    v = jnp.var(x, axis=axis, keepdims=True)
    return (x - m) / jnp.sqrt(v + eps)

def _scatter_add(tgt, idx, src, axis=0):
    return tgt.at[idx].add(src)

def _segment_sum(src, seg, n):
    return jax.ops.segment_sum(src, seg, n)
kernel_name = 'mk_conv_preact_d1_conv_nchw256_r4_735293'

def setup_inputs(seed: int=0):
    np.random.seed(seed)
    _w = jnp.asarray

    def _rec_inputs():
        import jax
        import jax.numpy as jnp
        _gk = jax.random.key(seed)
        x = -0.0002091 + 1 * jax.random.normal(jax.random.fold_in(_gk, 1), (32, 64, 56, 56), jnp.float32)
        return x
    x = _rec_inputs()

    def _L0_conv_setup():
        import jax, jax.numpy as jnp
        import numpy as np
        B, CIN, COUT, H, W, K, KH, KW = (32, 64, 64, 56, 56, 4, 3, 3)
        STRIDE, PAD = ((1, 1), [(1, 1), (1, 1)])
        key = jax.random.key(seed)
        ks = jax.random.split(key, 8)
        s_w = 1.0 / np.sqrt(CIN * KH * KW)
        return {'x': jax.random.normal(ks[0], (B, CIN, H, W), jnp.float32), 'weight': jax.random.normal(ks[1], (K, COUT, CIN, KH, KW), jnp.float32) * s_w, 'bias': jax.random.normal(ks[2], (K, COUT), jnp.float32) * s_w, 'fc1_w': jax.random.normal(ks[3], (K, CIN), jnp.float32) / np.sqrt(CIN), 'fc1_b': jax.random.normal(ks[4], (K,), jnp.float32) * 0.01, 'fc2_w': jax.random.normal(ks[5], (K, K), jnp.float32) / np.sqrt(K), 'fc2_b': jax.random.normal(ks[6], (K,), jnp.float32) * 0.01}
    _L0_conv_all = _L0_conv_setup()
    _L0_conv_in = {k: v for k, v in _L0_conv_all.items() if k in ('weight', 'bias', 'fc1_w', 'fc1_b', 'fc2_w', 'fc2_b')}
    del _L0_conv_all
    return {'x': x, 'L0_conv_weight': _L0_conv_in['weight'], 'L0_conv_bias': _L0_conv_in['bias'], 'L0_conv_fc1_w': _L0_conv_in['fc1_w'], 'L0_conv_fc1_b': _L0_conv_in['fc1_b'], 'L0_conv_fc2_w': _L0_conv_in['fc2_w'], 'L0_conv_fc2_b': _L0_conv_in['fc2_b']}

def reference(x, L0_conv_weight, L0_conv_bias, L0_conv_fc1_w, L0_conv_fc1_b, L0_conv_fc2_w, L0_conv_fc2_b):
    import jax
    import jax.numpy as jnp

    def _L0_conv_ref(x, weight, bias, fc1_w, fc1_b, fc2_w, fc2_b):
        import jax, jax.numpy as jnp
        import numpy as np
        B, CIN, COUT, H, W, K, KH, KW = (32, 64, 64, 56, 56, 4, 3, 3)
        STRIDE, PAD = ((1, 1), [(1, 1), (1, 1)])
        pooled = x.mean(axis=(2, 3))
        a = jax.nn.relu(jnp.einsum('bc,kc->bk', pooled, fc1_w) + fc1_b)
        att = jax.nn.softmax(jnp.einsum('bk,jk->bj', a, fc2_w) + fc2_b, axis=1)
        agg_w = jnp.einsum('bk,koihw->boihw', att, weight)
        agg_b = att @ bias

        def conv_one(xi, wi):
            return jax.lax.conv_general_dilated(xi[None], wi, window_strides=STRIDE, padding=PAD, dimension_numbers=('NCHW', 'OIHW', 'NCHW'))[0]
        out = jax.vmap(conv_one)(x, agg_w)
        return out + agg_b[:, :, None, None]

    def _gn(v, G=32, eps=1e-05):
        B_, C_, H_, W_ = v.shape
        g = v.reshape(B_, G, C_ // G, H_, W_)
        m = jnp.mean(g, axis=(2, 3, 4), keepdims=True)
        s = jnp.var(g, axis=(2, 3, 4), keepdims=True)
        return ((g - m) / jnp.sqrt(s + eps)).reshape(v.shape)

    def _ln_c(v, eps=1e-06):
        m = jnp.mean(v, axis=1, keepdims=True)
        s = jnp.var(v, axis=1, keepdims=True)
        return (v - m) / jnp.sqrt(s + eps)

    def _ln_t(v, eps=1e-05):
        m = jnp.mean(v, axis=-1, keepdims=True)
        s = jnp.var(v, axis=-1, keepdims=True)
        return (v - m) / jnp.sqrt(s + eps)

    def _to_tokens(v):
        B_, C_, H_, W_ = v.shape
        return v.reshape(B_, C_, H_ * W_).transpose(0, 2, 1)

    def _from_tokens(t, like):
        B_, C_, H_, W_ = like.shape
        return t.transpose(0, 2, 1).reshape(B_, C_, H_, W_)
    x = x + _L0_conv_ref(_gn(x), L0_conv_weight, L0_conv_bias, L0_conv_fc1_w, L0_conv_fc1_b, L0_conv_fc2_w, L0_conv_fc2_b)
    return x

_drawn_inputs = setup_inputs


def setup_inputs(seed=0):
    import zlib

    import numpy as np

    out = dict(_drawn_inputs(seed))
    spreads = {}
    factors = {'L0_conv_bias': 3.014,
     'L0_conv_fc1_w': 8.0,
     'L0_conv_fc1_b': 8.0,
     'L0_conv_fc2_w': 8.0,
     'L0_conv_fc2_b': 8.0}
    for name, (base, spread) in spreads.items():
        noise = np.random.default_rng([zlib.crc32(name.encode()), seed]).standard_normal(out[name].shape)
        drawn = base * np.exp(spread * noise) if base else spread * noise
        out[name] = jnp.asarray(drawn.astype(out[name].dtype))
    for name, factor in factors.items():
        out[name] = (out[name] * factor).astype(out[name].dtype)
    return out
```

```python
import concourse.bass as bass
from concourse import mybir
from concourse.alu_op_type import AluOpType as ALU
from contextlib import ExitStack

B, C, H, W, K, TAPS = 32, 64, 56, 56, 4, 9
PAIRS = B // 2
P = 2 * C
PIX = H * W
PW = W + 2
PAD = (H + 2) * PW
ROWS = 8
GROUPS = H // ROWS
GN = ROWS * W
TOP = 4 * GN
TAP_ORDER = (0, 1, 2, 6, 8, 3, 4, 5, 7)
CENTRE = TAP_ORDER.index(4)
LO_TAPS = 5
XSCALE = 512.0
WLIMIT = 32000.0
EPS = 1e-5
FC1, BIAS, B1, FC2, B2 = 0, K, 2 * K, 3 * K, 3 * K + K * K
SMALL = B2 + K
W_SEM = 16 * 8
H_SEM = 16 * 4
L_SEM = 16 * 2
O_SEM = 16 * 2


def dynamic_conv(nc, x, w_t, small, out):
    fp32, fp16 = mybir.dt.float32, mybir.dt.float16
    ACT, AX = mybir.ActivationFunctionType, mybir.AxisListType

    x_d = x.rearrange("(p i) c h w -> p (i c) (h w)", i=2)
    out_d = out.rearrange("(p i) c h w -> p (i c) (h w)", i=2)

    ctx = ExitStack()
    with ctx:
        def sb(name, shape, dt=fp32):
            return ctx.enter_context(nc.sbuf_tensor(name, shape, dt))

        def sem(name):
            return ctx.enter_context(nc.semaphore(name))

        x_sb = [sb(f"x{i}", [P, PIX]) for i in range(2)]
        o_sb = [sb(f"o{i}", [P, PIX]) for i in range(2)]
        xh = sb("xh", [P, PAD], fp16)
        xl = sb("xl", [P, PAD], fp16)
        LOW, BELOW, RIGHT = range(3)
        mov = [[sb(f"mov{i}{m}", [P, 3, PAD], fp16) for m in range(2)] for i in range(2)]
        w_sb = sb("w_sb", [P, K, TAPS * C])
        mix = sb("mix", [P, TAPS * C])
        wh = sb("wh", [P, TAPS * C], fp16)
        wl = sb("wl", [P, TAPS * C], fp16)
        st_hi = [[sb(f"st_hi{i}{m}", [P, TAPS * C], fp16) for m in range(2)] for i in range(2)]
        st_lo = [[sb(f"st_lo{i}{m}", [P, LO_TAPS * C], fp16) for m in range(2)] for i in range(2)]
        small_sb = sb("small_sb", [P, SMALL])
        group = sb("group", [P, P])
        image = sb("image", [P, P])
        ones = sb("ones", [P, P])
        eye = sb("eye", [P, C])
        neg_half = sb("neg_half", [P, 1])
        wpart = sb("wpart", [P, 1])
        wmax = sb("wmax", [P, 1])
        stats = sb("stats", [P, GROUPS, 6])
        mv = sb("mv", [P, 2])
        gm = sb("gm", [P, 2])
        dev = sb("dev", [P, 1])
        gvar = sb("gvar", [P, 1])
        var = sb("var", [P, 1])
        root = sb("root", [P, 1])
        newton = sb("newton", [P, 2])
        rstd = sb("rstd", [P, 1])
        sums = sb("sums", [P, K + 1])
        hid = sb("hid", [P, K])
        prod = sb("prod", [P, K, K])
        logit = sb("logit", [P, K])
        logit_b = sb("logit_b", [P, K])
        nmax = sb("nmax", [P, 1])
        ex = sb("ex", [P, K])
        exsum = sb("exsum", [P, 1])
        rsum = sb("rsum", [P, 1])
        bprod = sb("bprod", [P, K])
        bsum = sb("bsum", [P, 1])
        wrange = sb("wrange", [P, 1])
        wrecip = sb("wrecip", [P, 1])
        att = [sb(f"att{i}", [P, K]) for i in range(2)]
        std = [sb(f"std{i}", [P, 1]) for i in range(2)]
        xsc = [sb(f"xsc{i}", [P, 1]) for i in range(2)]
        xof = [sb(f"xof{i}", [P, 1]) for i in range(2)]
        wsc = [sb(f"wsc{i}", [P, 1]) for i in range(2)]
        par = [sb(f"par{i}", [P, 2]) for i in range(2)]
        out_par = [sb(f"out_par{i}", [P, 2]) for i in range(2)]

        acc = [ctx.enter_context(nc.psum_tensor(f"acc{t}", [P, 512], fp32)) for t in range(GROUPS)]
        tiny = ctx.enter_context(nc.psum_tensor("tiny", [P, 512], fp32))

        s_const = sem("s_const")
        s_sel = sem("s_sel")
        s_zero = sem("s_zero")
        s_wpart = sem("s_wpart")
        s_wmax = sem("s_wmax")
        x_top = [sem(f"x_top{i}") for i in range(2)]
        x_bot = [sem(f"x_bot{i}") for i in range(2)]
        dch = sem("dch")
        s_mv = sem("s_mv")
        s_gm = sem("s_gm")
        s_var = sem("s_var")
        s_root = sem("s_root")
        s_sums = sem("s_sums")
        s_fc1 = sem("s_fc1")
        s_logit = sem("s_logit")
        s_exp = sem("s_exp")
        s_par = sem("s_par")
        s_mix0 = sem("s_mix0")
        s_part = sem("s_part")
        s_mix = sem("s_mix")
        s_wh = sem("s_wh")
        s_wl = sem("s_wl")
        s_xn = sem("s_xn")
        s_xh = sem("s_xh")
        s_xl = sem("s_xl")
        s_same = sem("s_same")
        w_in = [sem(f"w_in{i}") for i in range(2)]
        h_in = [sem(f"h_in{i}") for i in range(2)]
        l_in = [sem(f"l_in{i}") for i in range(2)]
        s_conv = sem("s_conv")
        s_outp = sem("s_outp")
        s_res = sem("s_res")
        stored = [sem(f"stored{i}") for i in range(2)]

        def plane(t):
            return t.rearrange("p (r c) -> p r c", c=PW)

        def inner(t, half):
            r0 = half * H // 2
            return plane(t)[:, 1 + r0:1 + r0 + H // 2, 1:1 + W]

        def rows_of(t, half):
            return t.rearrange("p (r c) -> p r c", c=W)[:, half * H // 2:(half + 1) * H // 2, :]

        halves = (slice(0, C), slice(C, P))

        block = ctx.enter_context(nc.Block())

        @block.sync
        def _(sp):
            def load(p, i):
                sp.dma_start(x_sb[i][:, 0:TOP], x_d[p, :, 0:TOP]).then_inc(x_top[i], 16)
                sp.dma_start(x_sb[i][:, TOP:PIX], x_d[p, :, TOP:PIX]).then_inc(x_bot[i], 16)

            def spread_weights(p, i, free=True):
                sp.wait_ge(s_wh, p + 1)
                if free:
                    sp.wait_ge(s_conv, GROUPS * (p - 1))
                for m in range(2):
                    for half in halves:
                        sp.dma_start(st_hi[i][m][half, :], wh[halves[m], :]).then_inc(w_in[i], 16)
                sp.wait_ge(s_wl, p + 1)
                for m in range(2):
                    own, other = halves[m], halves[1 - m]
                    sp.dma_start(st_lo[i][m][own, :], wl[own, 0:LO_TAPS * C]).then_inc(w_in[i], 16)
                    sp.dma_start(st_lo[i][m][other, 0:(LO_TAPS - 1) * C],
                                 wl[own, LO_TAPS * C:TAPS * C]).then_inc(w_in[i], 16)

            def spread_high(p, i):
                sp.wait_ge(s_xh, 2 * (p + 1))
                for kind, shift in ((BELOW, PW), (RIGHT, 1)):
                    for m in range(2):
                        own, other = halves[m], halves[1 - m]
                        sp.dma_start(mov[i][m][other, kind, 0:PAD - shift],
                                     xh[own, shift:PAD]).then_inc(h_in[i], 16)

            def spread_low(p, i):
                sp.wait_ge(s_xl, 2 * (p + 1))
                for m in range(2):
                    own, other = halves[m], halves[1 - m]
                    sp.dma_start(mov[i][m][other, LOW, :], xl[own, :]).then_inc(l_in[i], 16)

            def store_top(p, i):
                sp.wait_ge(s_res, GROUPS * p + TOP // GN)
                sp.dma_start(out_d[p, :, 0:TOP], o_sb[i][:, 0:TOP]).then_inc(stored[i], 16)

            def store_bottom(p, i):
                sp.wait_ge(s_res, GROUPS * (p + 1))
                sp.dma_start(out_d[p, :, TOP:PIX], o_sb[i][:, TOP:PIX]).then_inc(stored[i], 16)

            def step(p, i, more, free=True):
                spread_weights(p, i, free)
                spread_high(p, i)
                store_top(p - 1, 1 - i)
                spread_low(p, i)
                if more:
                    load(p + 2, i)
                store_bottom(p - 1, 1 - i)

            sp.dma_start(x_sb[0][:, 0:TOP], x_d[0, :, 0:TOP]).then_inc(x_top[0], 16)
            sp.dma_start(x_sb[0][:, TOP:PIX], x_d[0, :, TOP:PIX]).then_inc(x_bot[0], 16)
            sp.dma_start(small_sb[:], small).then_inc(s_const, 16)
            for half in halves:
                sp.dma_start(w_sb[half, :, :], w_t).then_inc(s_const, 16)
            load(1, 1)
            spread_weights(0, 0, free=False)
            spread_high(0, 0)
            spread_low(0, 0)
            load(2, 0)
            step(1, 1, True, free=False)
            with sp.Fori(1, PAIRS // 2 - 1) as q:
                step(2 * q, 0, True)
                step(2 * q + 1, 1, True)
            step(PAIRS - 2, 0, False)
            step(PAIRS - 1, 1, False)
            store_top(PAIRS - 1, 1)
            store_bottom(PAIRS - 1, 1)
            for i in range(2):
                sp.wait_ge(stored[i], O_SEM * PAIRS // 2)

        @block.gpsimd
        def _(pool):
            nc.gpsimd.memset(group[:], 0.5)
            nc.gpsimd.memset(image[:], 1.0)
            nc.gpsimd.memset(ones[:], 1.0)
            nc.gpsimd.memset(eye[:], 0.0)
            nc.gpsimd.memset(neg_half[:], -0.5).then_inc(s_sel, 1)
            pool.wait_ge(s_sel, 1)
            pairs_of = group[:].rearrange("k (g j) -> k g j", j=2)
            nc.gpsimd.affine_select(out=pairs_of, in_=pairs_of, compare_op=ALU.is_ge, fill=0.0, base=0,
                                    pattern=[[-2, P // 2], [0, 2]], channel_multiplier=1).then_inc(s_sel, 1)
            pool.wait_ge(s_sel, 2)
            nc.gpsimd.affine_select(out=pairs_of, in_=pairs_of, compare_op=ALU.is_ge, fill=0.0, base=1,
                                    pattern=[[2, P // 2], [0, 2]], channel_multiplier=-1).then_inc(s_sel, 1)
            low = image[:, 0:C]
            nc.gpsimd.affine_select(out=low, in_=low, compare_op=ALU.is_ge, fill=0.0, base=C - 1,
                                    pattern=[[0, C]], channel_multiplier=-1)
            high = image[:, C:P]
            nc.gpsimd.affine_select(out=high, in_=high, compare_op=ALU.is_ge, fill=0.0, base=-C,
                                    pattern=[[0, C]], channel_multiplier=1)
            nc.gpsimd.affine_select(out=eye[:], in_=eye[:], compare_op=ALU.not_equal, fill=1.0, base=0,
                                    pattern=[[-1, C]], channel_multiplier=1).then_inc(s_sel, 1)
            pool.wait_ge(s_sel, 4)
            nc.gpsimd.affine_select(out=eye[:], in_=eye[:], compare_op=ALU.not_equal, fill=1.0, base=-C,
                                    pattern=[[-1, C]], channel_multiplier=1).then_inc(s_sel, 1)
            pool.wait_ge(s_wpart, 1)
            nc.gpsimd.partition_all_reduce(wmax[:], wpart[:], P, bass.bass_isa.ReduceOp.max).then_inc(s_wmax, 1)
            with pool.Fori(0, PAIRS) as p:
                pool.wait_ge(s_var, p + 1)
                nc.gpsimd.tensor_tensor(root[:], var[:], neg_half[:], ALU.pow).then_inc(s_root, 1)

        @block.vector
        def _(dve):
            LINKS = 17

            def link(n, ins):
                ins.then_inc(dch, 1)
                dve.wait_ge(dch, n)

            def channel_stats(p, i, nth):
                n = LINKS * p
                for t in range(GROUPS):
                    if t == 0:
                        dve.wait_ge(x_top[i], 16 * nth)
                    if t == TOP // GN:
                        dve.wait_ge(x_bot[i], 16 * nth)
                    last = nc.vector.bn_stats(stats[:, t, :], x_sb[i][:, t * GN:(t + 1) * GN])
                link(n + 1, last)

            def channel_moments():
                nc.vector.bn_aggr(mv[:], stats[:]).then_inc(s_mv, 1)

            def group_stats(p, i):
                n = LINKS * p
                dve.wait_ge(s_gm, p + 1)
                link(n + 2, nc.vector.tensor_copy(gm[:], tiny[:, 0:2]))
                link(n + 3, nc.vector.tensor_tensor(dev[:], mv[:, 0:1], gm[:, 0:1], ALU.subtract))
                link(n + 4, nc.vector.scalar_tensor_tensor(out=gvar[:], in0=dev[:], scalar=dev[:], in1=gm[:, 1:2],
                                                           op0=ALU.mult, op1=ALU.add))
                nc.vector.tensor_scalar(var[:], gvar[:], EPS, None, ALU.add).then_inc(s_var, 1)
                dve.wait_ge(s_root, p + 1)
                link(n + 5, nc.vector.scalar_tensor_tensor(out=newton[:, 0:1], in0=root[:], scalar=root[:],
                                                           in1=var[:], op0=ALU.mult, op1=ALU.mult))
                link(n + 6, nc.vector.tensor_scalar(newton[:, 1:2], newton[:, 0:1], -0.5, 1.5, ALU.mult, ALU.add))
                link(n + 7, nc.vector.tensor_tensor(rstd[:], root[:], newton[:, 1:2], ALU.mult))
                nc.vector.tensor_scalar(std[i][:], var[:], rstd[:], None, ALU.mult)
                nc.vector.tensor_scalar(sums[:, K:K + 1], var[:], rstd[:], None, ALU.mult)
                nc.vector.tensor_scalar(sums[:, 0:K], small_sb[:, FC1:FC1 + K], dev[:], rstd[:],
                                        ALU.mult, ALU.mult).then_inc(s_sums, 1)
                nc.vector.tensor_scalar(xsc[i][:], rstd[:], XSCALE, None, ALU.mult)
                nc.vector.tensor_scalar(xof[i][:], gm[:, 0:1], rstd[:], -XSCALE, ALU.mult, ALU.mult)

            def logits(p, i):
                n = LINKS * p
                dve.wait_ge(s_fc1, p + 1)
                nc.vector.tensor_scalar(wrange[:], tiny[:, 2 + K:3 + K], wmax[:], None, ALU.add)
                link(n + 8, nc.vector.tensor_tensor(hid[:], tiny[:, 2:2 + K], small_sb[:, B1:B1 + K], ALU.add))
                fc2 = small_sb[:, FC2:FC2 + K * K].rearrange("p (j k) -> p j k", k=K)
                link(n + 9, nc.vector.scalar_tensor_tensor(
                    out=prod[:], in0=hid[:].unsqueeze(1).to_broadcast([P, K, K]), scalar=0.0, in1=fc2,
                    op0=ALU.max, op1=ALU.mult))
                link(n + 10, nc.vector.tensor_reduce(logit[:], prod[:], AX.X, ALU.add))
                link(n + 11, nc.vector.tensor_tensor(logit_b[:], logit[:], small_sb[:, B2:B2 + K], ALU.add))
                nc.vector.tensor_reduce(nmax[:], logit_b[:], AX.X, ALU.max, negate=True).then_inc(s_logit, 1)
                link(n + 12, nc.vector.reciprocal(wrecip[:], wrange[:]))
                nc.vector.tensor_scalar(wsc[i][:], wrecip[:], WLIMIT, None, ALU.mult)
                nc.vector.tensor_scalar(par[i][:, 0:1], wrange[:], 1.0 / (WLIMIT * XSCALE), None, ALU.mult)

            def softmax(p, i):
                n = LINKS * p
                dve.wait_ge(s_exp, p + 1)
                link(n + 13, nc.vector.tensor_reduce(exsum[:], ex[:], AX.X, ALU.add))
                link(n + 14, nc.vector.reciprocal(rsum[:], exsum[:]))
                link(n + 15, nc.vector.tensor_scalar(att[i][:], ex[:], rsum[:], None, ALU.mult))
                link(n + 16, nc.vector.tensor_tensor(bprod[:], att[i][:], small_sb[:, BIAS:BIAS + K], ALU.mult))
                link(n + 17, nc.vector.tensor_reduce(bsum[:], bprod[:], AX.X, ALU.add))
                nc.vector.tensor_tensor(par[i][:, 1:2], bsum[:], gm[:, 0:1], ALU.add).then_inc(s_par, 1)

            def mixture(p, i):
                dve.wait_ge(s_mix0, p + 1)
                for k in range(1, K):
                    nc.vector.scalar_tensor_tensor(out=mix[:], in0=w_sb[:, k, :], scalar=att[i][:, k:k + 1],
                                                   in1=mix[:], op0=ALU.mult, op1=ALU.add).then_inc(s_part, 1)
                    dve.wait_ge(s_part, (K - 1) * p + k)
                centre = mix[:, CENTRE * C:(CENTRE + 1) * C]
                nc.vector.scalar_tensor_tensor(out=centre, in0=eye[:], scalar=std[i][:], in1=centre,
                                               op0=ALU.mult, op1=ALU.add).then_inc(s_mix, 1)

            def low_weights(p, i, before):
                dve.wait_ge(s_wh, p + 1)
                if before is not None:
                    dve.wait_ge(w_in[1 - i], W_SEM * before)
                nc.vector.scalar_tensor_tensor(out=wl[:], in0=mix[:], scalar=wsc[i][:], in1=wh[:],
                                               op0=ALU.mult, op1=ALU.subtract).then_inc(s_wl, 1)

            def low_inputs(p, i, before):
                if before is not None:
                    dve.wait_ge(l_in[1 - i], L_SEM * before)
                for half in range(2):
                    dve.wait_ge(s_xh, 2 * p + half + 1)
                    nc.vector.tensor_tensor(inner(xl, half), rows_of(x_sb[i], half),
                                            inner(xh, half), ALU.subtract).then_inc(s_xl, 1)

            def keep_params(p, i, free):
                if free:
                    dve.wait_ge(s_res, GROUPS * (p - 1))
                nc.vector.tensor_copy(out_par[i][:], par[i][:]).then_inc(s_outp, 1)

            def copy_high(p, i, m, free):
                if free:
                    dve.wait_ge(s_conv, GROUPS * (p - 1))
                own = halves[m]
                nc.vector.tensor_copy(mov[i][m][own, :, :],
                                      xh[own, :].unsqueeze(1).to_broadcast([C, 3, PAD])).then_inc(s_same, 1)

            def step(p, i, nth, before, free=True, more=True):
                mixture(p, i)
                low_weights(p, i, before)
                if more:
                    channel_stats(p + 1, 1 - i, nth)
                keep_params(p, i, free)
                if more:
                    channel_moments()
                low_inputs(p, i, before)
                if more:
                    group_stats(p + 1, 1 - i)
                copy_high(p, i, 0, free)
                if more:
                    logits(p + 1, 1 - i)
                copy_high(p, i, 1, free)
                if more:
                    softmax(p + 1, 1 - i)

            nc.vector.memset(xh[:].bitcast(fp32), 0.0)
            nc.vector.memset(xl[:].bitcast(fp32), 0.0)
            for i in range(2):
                for m in range(2):
                    last = nc.vector.memset(st_lo[i][m][halves[1 - m], (LO_TAPS - 1) * C:LO_TAPS * C], 0.0)
            last.then_inc(s_zero, 1)
            dve.wait_ge(s_const, 16 * 3)
            nc.vector.tensor_reduce(wpart[:], w_sb[:], AX.XY, ALU.max,
                                    apply_absolute_value=True).then_inc(s_wpart, 1)
            channel_stats(0, 0, 1)
            channel_moments()
            group_stats(0, 0)
            dve.wait_ge(s_wmax, 1)
            logits(0, 0)
            softmax(0, 0)
            step(0, 0, 1, None, free=False)
            step(1, 1, 2, 1, free=False)
            with dve.Fori(1, PAIRS // 2 - 1) as q:
                step(2 * q, 0, q + 1, q)
                step(2 * q + 1, 1, q + 2, q + 1)
            step(PAIRS - 2, 0, PAIRS // 2, PAIRS // 2 - 1)
            step(PAIRS - 1, 1, None, PAIRS // 2, more=False)

        @block.scalar
        def _(act):
            def normalise(p, i):
                act.wait_ge(s_par, p + 1)
                for half in range(2):
                    v = rows_of(x_sb[i], half)
                    nc.scalar.activation(v, v, ACT.Identity, bias=xof[i][:], scale=xsc[i][:]).then_inc(s_xn, 1)

            def first_expert(p, i, free):
                act.wait_ge(s_par, p + 1)
                if free:
                    act.wait_ge(s_wl, p)
                nc.scalar.activation(mix[:], w_sb[:, 0, :], ACT.Copy, scale=att[i][:, 0:1]).then_inc(s_mix0, 1)

            def high_weights(p, i, before):
                act.wait_ge(s_mix, p + 1)
                if before is not None:
                    act.wait_ge(w_in[1 - i], W_SEM * before)
                nc.scalar.activation(wh[:], mix[:], ACT.Copy, scale=wsc[i][:]).then_inc(s_wh, 1)

            def high_inputs(p, i, before):
                if before is not None:
                    act.wait_ge(s_same, 2 * p)
                    act.wait_ge(h_in[1 - i], H_SEM * before)
                for half in range(2):
                    act.wait_ge(s_xn, 2 * p + half + 1)
                    nc.scalar.activation(inner(xh, half), rows_of(x_sb[i], half), ACT.Copy).then_inc(s_xh, 1)

            def exponentials(p):
                act.wait_ge(s_logit, p + 1)
                nc.scalar.activation(ex[:], logit_b[:], ACT.Exp, bias=nmax[:]).then_inc(s_exp, 1)

            def results(p, i, t, before):
                if t == 0:
                    act.wait_ge(s_outp, p + 1)
                    if before is not None:
                        act.wait_ge(stored[i], O_SEM * before)
                act.wait_ge(s_conv, GROUPS * p + t + 1)
                nc.scalar.activation(o_sb[i][:, t * GN:(t + 1) * GN], acc[t][:, 0:GN], ACT.Identity,
                                     bias=out_par[i][:, 1:2], scale=out_par[i][:, 0:1]).then_inc(s_res, 1)

            def step(p, i, before, res_before=None, last=True, more=True):
                first_expert(p, i, before is not None)
                normalise(p, i)
                high_weights(p, i, before)
                high_inputs(p, i, before)
                for t in range(GROUPS):
                    if more and t == (GROUPS - 1 if last else 0):
                        exponentials(p + 1)
                    if last:
                        results(p - 1, 1 - i, t, res_before)

            act.wait_ge(s_zero, 1)
            exponentials(0)
            step(0, 0, None, last=False)
            step(1, 1, 1)
            with act.Fori(1, PAIRS // 2 - 1) as q:
                step(2 * q, 0, q, q - 1)
                step(2 * q + 1, 1, q + 1, q)
            step(PAIRS - 2, 0, PAIRS // 2 - 1, PAIRS // 2 - 2)
            step(PAIRS - 1, 1, PAIRS // 2, PAIRS // 2 - 1, more=False)
            for t in range(GROUPS):
                results(PAIRS - 1, 1, t, PAIRS // 2 - 1)

        @block.tensor
        def _(pe):
            def group_means(p):
                pe.wait_ge(s_mv, p + 1)
                nc.tensor.matmul(tiny[:, 0:2], group[:], mv[:], start=True, stop=True).then_inc(s_gm, 1)

            def image_sums(p):
                pe.wait_ge(s_sums, p + 1)
                nc.tensor.matmul(tiny[:, 2:3 + K], image[:], sums[:], start=True, stop=True).then_inc(s_fc1, 1)

            def convolve(p, i, t, free):
                if free:
                    pe.wait_ge(s_res, GROUPS * (p - 1) + t + 1)
                blocks = [(st_hi, n, LOW, tap // 3, tap % 3) for n, tap in enumerate(TAP_ORDER)]
                blocks += [(st_lo, n, BELOW, 0, n) for n in range(3)]
                blocks += [(st_lo, 3, RIGHT, 2, 0), (st_lo, 4, LOW, 2, 2)]
                for n, (st, slot, kind, kh, kw) in enumerate(blocks):
                    for m in range(2):
                        r0 = t * ROWS + kh
                        last = nc.tensor.matmul(acc[t][halves[m], 0:GN], st[i][m][:, slot * C:(slot + 1) * C],
                                                plane(mov[i][m][:, kind, :])[:, r0:r0 + ROWS, kw:kw + W],
                                                start=n == 0, stop=n == len(blocks) - 1)
                last.then_inc(s_conv, 1)

            def step(p, i, nth, free=True, more=True):
                pe.wait_ge(w_in[i], W_SEM * nth)
                pe.wait_ge(h_in[i], H_SEM * nth)
                pe.wait_ge(l_in[i], L_SEM * nth)
                pe.wait_ge(s_same, 2 * (p + 1))
                for t in range(GROUPS):
                    convolve(p, i, t, free)
                    if more and t == 2:
                        group_means(p + 2)
                    if more and t == 4:
                        image_sums(p + 2)

            pe.wait_ge(s_sel, 5)
            for p in range(2):
                group_means(p)
                image_sums(p)
            step(0, 0, 1, free=False)
            step(1, 1, 1)
            with pe.Fori(1, PAIRS // 2 - 1) as q:
                step(2 * q, 0, q + 1)
                step(2 * q + 1, 1, q + 1)
            step(PAIRS - 2, 0, PAIRS // 2, more=False)
            step(PAIRS - 1, 1, PAIRS // 2, more=False)


def kernel(x, L0_conv_weight, L0_conv_bias, L0_conv_fc1_w, L0_conv_fc1_b, L0_conv_fc2_w, L0_conv_fc2_b):
    import numpy as np
    import concourse.bacc as bacc
    from concourse.bass_utils import run_bass_kernel_spmd

    w = np.asarray(L0_conv_weight).reshape(K, C, C, TAPS)[..., list(TAP_ORDER)]
    arrays = {
        "x": np.ascontiguousarray(x),
        "w_t": np.ascontiguousarray(w.transpose(2, 0, 3, 1).reshape(C, K, TAPS * C)),
        "small": np.ascontiguousarray(np.concatenate([
            np.tile(np.asarray(L0_conv_fc1_w).T, (2, 1)),
            np.tile(np.asarray(L0_conv_bias).T, (2, 1)),
            np.tile(np.asarray(L0_conv_fc1_b)[None], (P, 1)),
            np.tile(np.asarray(L0_conv_fc2_w).reshape(1, K * K), (P, 1)),
            np.tile(np.asarray(L0_conv_fc2_b)[None], (P, 1)),
        ], axis=1)),
    }
    nc = bacc.Bacc("TRN2", target_bir_lowering=False, num_devices=1)
    ins = [nc.dram_tensor(n, a.shape, mybir.dt.from_np(a.dtype), kind="ExternalInput").ap()
           for n, a in arrays.items()]
    out = nc.dram_tensor("out", (B, C, H, W), mybir.dt.float32, kind="ExternalOutput").ap()
    dynamic_conv(nc, *ins, out)
    r = run_bass_kernel_spmd(nc, [arrays], core_ids=[0])
    return r.results[0]["out"]
```

```python
import concourse.bass as bass
from concourse import mybir
from concourse.alu_op_type import AluOpType as ALU
from contextlib import ExitStack

B, C, H, W, K, TAPS = 32, 64, 56, 56, 4, 9
PAIRS = B // 2
P = 2 * C
PIX = H * W
PW = W + 2
PAD = (H + 2) * PW
ROWS = 8
GROUPS = H // ROWS
GN = ROWS * W
TOP = 4 * GN
TAP_ORDER = (0, 1, 2, 6, 8, 3, 4, 5, 7)
CENTRE = TAP_ORDER.index(4)
LO_TAPS = 5
XSCALE = 512.0
WLIMIT = 32000.0
EPS = 1e-5
FC1, BIAS, B1, FC2, B2 = 0, K, 2 * K, 3 * K, 3 * K + K * K
SMALL = B2 + K
W_SEM = 16 * 8
H_SEM = 16 * 4
L_SEM = 16 * 2
O_SEM = 16 * 2


def dynamic_conv(nc, x, w_t, small, out):
    fp32, fp16 = mybir.dt.float32, mybir.dt.float16
    ACT, AX = mybir.ActivationFunctionType, mybir.AxisListType

    x_d = x.rearrange("(p i) c h w -> p (i c) (h w)", i=2)
    out_d = out.rearrange("(p i) c h w -> p (i c) (h w)", i=2)

    ctx = ExitStack()
    with ctx:
        def sb(name, shape, dt=fp32):
            return ctx.enter_context(nc.sbuf_tensor(name, shape, dt))

        def sem(name):
            return ctx.enter_context(nc.semaphore(name))

        x_sb = [sb(f"x{i}", [P, PIX]) for i in range(2)]
        o_sb = [sb(f"o{i}", [P, PIX]) for i in range(2)]
        xh = sb("xh", [P, PAD], fp16)
        xl = sb("xl", [P, PAD], fp16)
        LOW, BELOW, RIGHT = range(3)
        mov = [[sb(f"mov{i}{m}", [P, 3, PAD], fp16) for m in range(2)] for i in range(2)]
        w_sb = sb("w_sb", [P, K, TAPS * C])
        mix = sb("mix", [P, TAPS * C])
        wh = sb("wh", [P, TAPS * C], fp16)
        wl = sb("wl", [P, TAPS * C], fp16)
        st_hi = [[sb(f"st_hi{i}{m}", [P, TAPS * C], fp16) for m in range(2)] for i in range(2)]
        st_lo = [[sb(f"st_lo{i}{m}", [P, LO_TAPS * C], fp16) for m in range(2)] for i in range(2)]
        small_sb = sb("small_sb", [P, SMALL])
        group = sb("group", [P, P])
        image = sb("image", [P, P])
        ones = sb("ones", [P, P])
        eye = sb("eye", [P, C])
        CONSTS = (EPS, -0.5, 1.5, XSCALE, -XSCALE)
        consts = sb("consts", [P, len(CONSTS)])
        wpart = sb("wpart", [P, 1])
        wmax = sb("wmax", [P, 1])
        stats = sb("stats", [P, GROUPS, 6])
        mv = sb("mv", [P, 2])
        gm = sb("gm", [P, 2])
        dev = sb("dev", [P, 1])
        dev2 = sb("dev2", [P, 1])
        gvar = sb("gvar", [P, 1])
        pooled = sb("pooled", [P, 1])
        noff = sb("noff", [P, 1])
        var = sb("var", [P, 1])
        root = sb("root", [P, 1])
        newton = sb("newton", [P, 4])
        rstd = sb("rstd", [P, 1])
        sums = sb("sums", [P, K + 1])
        hid = sb("hid", [P, K])
        prod = sb("prod", [P, K, K])
        logit = sb("logit", [P, K])
        logit_b = sb("logit_b", [P, K])
        nmax = sb("nmax", [P, 1])
        ex = sb("ex", [P, K])
        exsum = sb("exsum", [P, 1])
        rsum = sb("rsum", [P, 1])
        bprod = sb("bprod", [P, K])
        bsum = sb("bsum", [P, 1])
        wrange = sb("wrange", [P, 1])
        wrecip = sb("wrecip", [P, 1])
        att = [sb(f"att{i}", [P, K]) for i in range(2)]
        std = [sb(f"std{i}", [P, 1]) for i in range(2)]
        xsc = [sb(f"xsc{i}", [P, 1]) for i in range(2)]
        xof = [sb(f"xof{i}", [P, 1]) for i in range(2)]
        wsc = [sb(f"wsc{i}", [P, 1]) for i in range(2)]
        par = [sb(f"par{i}", [P, 2]) for i in range(2)]
        out_par = [sb(f"out_par{i}", [P, 2]) for i in range(2)]

        acc = [ctx.enter_context(nc.psum_tensor(f"acc{t}", [P, 512], fp32)) for t in range(GROUPS)]
        tiny = ctx.enter_context(nc.psum_tensor("tiny", [P, 512], fp32))

        s_const = sem("s_const")
        s_sel = sem("s_sel")
        s_zero = sem("s_zero")
        s_wpart = sem("s_wpart")
        s_wmax = sem("s_wmax")
        x_top = [sem(f"x_top{i}") for i in range(2)]
        x_bot = [sem(f"x_bot{i}") for i in range(2)]
        dch = sem("dch")
        s_mv = sem("s_mv")
        s_gm = sem("s_gm")
        s_gcopy = sem("s_gcopy")
        pch = sem("pch")
        s_norm = sem("s_norm")
        s_sums = sem("s_sums")
        s_fc1 = sem("s_fc1")
        s_logit = sem("s_logit")
        s_exp = sem("s_exp")
        s_par = sem("s_par")
        s_part = sem("s_part")
        s_mix = sem("s_mix")
        s_wh = sem("s_wh")
        s_wl = sem("s_wl")
        s_xn = sem("s_xn")
        s_xh = sem("s_xh")
        s_xl = sem("s_xl")
        s_same = sem("s_same")
        w_in = [sem(f"w_in{i}") for i in range(2)]
        h_in = [sem(f"h_in{i}") for i in range(2)]
        l_in = [sem(f"l_in{i}") for i in range(2)]
        s_conv = sem("s_conv")
        s_outp = sem("s_outp")
        s_res = sem("s_res")
        stored = [sem(f"stored{i}") for i in range(2)]

        def const(value):
            n = CONSTS.index(value)
            return consts[:, n:n + 1]

        def plane(t):
            return t.rearrange("p (r c) -> p r c", c=PW)

        def inner(t, half):
            r0 = half * H // 2
            return plane(t)[:, 1 + r0:1 + r0 + H // 2, 1:1 + W]

        def rows_of(t, half):
            return t.rearrange("p (r c) -> p r c", c=W)[:, half * H // 2:(half + 1) * H // 2, :]

        halves = (slice(0, C), slice(C, P))

        block = ctx.enter_context(nc.Block())

        @block.sync
        def _(sp):
            def load(p, i):
                sp.dma_start(x_sb[i][:, 0:TOP], x_d[p, :, 0:TOP]).then_inc(x_top[i], 16)
                sp.dma_start(x_sb[i][:, TOP:PIX], x_d[p, :, TOP:PIX]).then_inc(x_bot[i], 16)

            def spread_weights(p, i):
                sp.wait_ge(s_wh, p + 1)
                for m in range(2):
                    for half in halves:
                        sp.dma_start(st_hi[i][m][half, :], wh[halves[m], :]).then_inc(w_in[i], 16)
                sp.wait_ge(s_wl, p + 1)
                for m in range(2):
                    own, other = halves[m], halves[1 - m]
                    sp.dma_start(st_lo[i][m][own, :], wl[own, 0:LO_TAPS * C]).then_inc(w_in[i], 16)
                    sp.dma_start(st_lo[i][m][other, 0:(LO_TAPS - 1) * C],
                                 wl[own, LO_TAPS * C:TAPS * C]).then_inc(w_in[i], 16)

            def spread_high(p, i, free):
                sp.wait_ge(s_xh, 2 * (p + 1))
                if free:
                    sp.wait_ge(s_conv, GROUPS * (p - 1))
                for kind, shift in ((BELOW, PW), (RIGHT, 1)):
                    for m in range(2):
                        own, other = halves[m], halves[1 - m]
                        sp.dma_start(mov[i][m][other, kind, 0:PAD - shift],
                                     xh[own, shift:PAD]).then_inc(h_in[i], 16)

            def spread_low(p, i):
                sp.wait_ge(s_xl, 2 * (p + 1))
                for m in range(2):
                    own, other = halves[m], halves[1 - m]
                    sp.dma_start(mov[i][m][other, LOW, :], xl[own, :]).then_inc(l_in[i], 16)

            def store_top(p, i):
                sp.wait_ge(s_res, GROUPS * p + TOP // GN)
                sp.dma_start(out_d[p, :, 0:TOP], o_sb[i][:, 0:TOP]).then_inc(stored[i], 16)

            def store_bottom(p, i):
                sp.wait_ge(s_res, GROUPS * (p + 1))
                sp.dma_start(out_d[p, :, TOP:PIX], o_sb[i][:, TOP:PIX]).then_inc(stored[i], 16)

            def step(p, i, more, free=True):
                spread_high(p, i, free)
                spread_low(p, i)
                if more:
                    load(p + 2, i)
                spread_weights(p, i)
                store_top(p - 1, 1 - i)
                store_bottom(p - 1, 1 - i)

            sp.dma_start(x_sb[0][:, 0:TOP], x_d[0, :, 0:TOP]).then_inc(x_top[0], 16)
            sp.dma_start(x_sb[0][:, TOP:PIX], x_d[0, :, TOP:PIX]).then_inc(x_bot[0], 16)
            sp.dma_start(small_sb[:], small).then_inc(s_const, 16)
            for half in halves:
                sp.dma_start(w_sb[half, :, :], w_t).then_inc(s_const, 16)
            load(1, 1)
            spread_high(0, 0, free=False)
            spread_low(0, 0)
            load(2, 0)
            spread_weights(0, 0)
            step(1, 1, True, free=False)
            with sp.Fori(1, PAIRS // 2 - 1) as q:
                step(2 * q, 0, True)
                step(2 * q + 1, 1, True)
            step(PAIRS - 2, 0, False)
            step(PAIRS - 1, 1, False)
            store_top(PAIRS - 1, 1)
            store_bottom(PAIRS - 1, 1)
            for i in range(2):
                sp.wait_ge(stored[i], O_SEM * PAIRS // 2)

        @block.gpsimd
        def _(pool):
            nc.gpsimd.memset(group[:], 0.5)
            nc.gpsimd.memset(image[:], 1.0)
            nc.gpsimd.memset(ones[:], 1.0)
            nc.gpsimd.memset(eye[:], 0.0)
            for n, value in enumerate(CONSTS):
                last = nc.gpsimd.memset(consts[:, n:n + 1], value)
            last.then_inc(s_sel, 1)
            pool.wait_ge(s_sel, 1)
            pairs_of = group[:].rearrange("k (g j) -> k g j", j=2)
            nc.gpsimd.affine_select(out=pairs_of, in_=pairs_of, compare_op=ALU.is_ge, fill=0.0, base=0,
                                    pattern=[[-2, P // 2], [0, 2]], channel_multiplier=1).then_inc(s_sel, 1)
            pool.wait_ge(s_sel, 2)
            nc.gpsimd.affine_select(out=pairs_of, in_=pairs_of, compare_op=ALU.is_ge, fill=0.0, base=1,
                                    pattern=[[2, P // 2], [0, 2]], channel_multiplier=-1).then_inc(s_sel, 1)
            low = image[:, 0:C]
            nc.gpsimd.affine_select(out=low, in_=low, compare_op=ALU.is_ge, fill=0.0, base=C - 1,
                                    pattern=[[0, C]], channel_multiplier=-1)
            high = image[:, C:P]
            nc.gpsimd.affine_select(out=high, in_=high, compare_op=ALU.is_ge, fill=0.0, base=-C,
                                    pattern=[[0, C]], channel_multiplier=1)
            nc.gpsimd.affine_select(out=eye[:], in_=eye[:], compare_op=ALU.not_equal, fill=1.0, base=0,
                                    pattern=[[-1, C]], channel_multiplier=1).then_inc(s_sel, 1)
            pool.wait_ge(s_sel, 4)
            nc.gpsimd.affine_select(out=eye[:], in_=eye[:], compare_op=ALU.not_equal, fill=1.0, base=-C,
                                    pattern=[[-1, C]], channel_multiplier=1).then_inc(s_sel, 1)
            pool.wait_ge(s_wpart, 1)
            nc.gpsimd.partition_all_reduce(wmax[:], wpart[:], P, bass.bass_isa.ReduceOp.max).then_inc(s_wmax, 1)

            CHAIN = 12

            def link(n, ins):
                ins.then_inc(pch, 1)
                pool.wait_ge(pch, n)

            def group_stats(p, i):
                n = CHAIN * p
                tt = nc.gpsimd.tensor_tensor
                pool.wait_ge(s_gcopy, p + 1)
                link(n + 1, tt(dev[:], mv[:, 0:1], gm[:, 0:1], ALU.subtract))
                link(n + 2, tt(dev2[:], dev[:], dev[:], ALU.mult))
                link(n + 3, tt(gvar[:], dev2[:], gm[:, 1:2], ALU.add))
                link(n + 4, tt(var[:], gvar[:], const(EPS), ALU.add))
                link(n + 5, tt(root[:], var[:], const(-0.5), ALU.pow))
                link(n + 6, tt(newton[:, 0:1], root[:], root[:], ALU.mult))
                link(n + 7, tt(newton[:, 1:2], newton[:, 0:1], var[:], ALU.mult))
                link(n + 8, tt(newton[:, 2:3], newton[:, 1:2], const(-0.5), ALU.mult))
                link(n + 9, tt(newton[:, 3:4], newton[:, 2:3], const(1.5), ALU.add))
                link(n + 10, tt(rstd[:], root[:], newton[:, 3:4], ALU.mult))
                tt(std[i][:], var[:], rstd[:], ALU.mult)
                tt(sums[:, K:K + 1], var[:], rstd[:], ALU.mult)
                tt(xsc[i][:], rstd[:], const(XSCALE), ALU.mult)
                link(n + 11, tt(pooled[:], dev[:], rstd[:], ALU.mult))
                tt(sums[:, 0:K], small_sb[:, FC1:FC1 + K], pooled[:].to_broadcast([P, K]),
                   ALU.mult).then_inc(s_sums, 1)
                link(n + 12, tt(noff[:], gm[:, 0:1], const(-XSCALE), ALU.mult))
                tt(xof[i][:], noff[:], rstd[:], ALU.mult).then_inc(s_norm, 1)

            pool.wait_ge(s_const, 16 * 3)
            with pool.Fori(0, PAIRS // 2) as q:
                group_stats(2 * q, 0)
                group_stats(2 * q + 1, 1)

        @block.vector
        def _(dve):
            LINKS = 11

            def link(n, ins):
                ins.then_inc(dch, 1)
                dve.wait_ge(dch, n)

            def channel_stats(p, i, nth):
                n = LINKS * p
                for t in range(GROUPS):
                    if t == 0:
                        dve.wait_ge(x_top[i], 16 * nth)
                    if t == TOP // GN:
                        dve.wait_ge(x_bot[i], 16 * nth)
                    last = nc.vector.bn_stats(stats[:, t, :], x_sb[i][:, t * GN:(t + 1) * GN])
                link(n + 1, last)

            def channel_moments():
                nc.vector.bn_aggr(mv[:], stats[:]).then_inc(s_mv, 1)

            def logits(p, i):
                n = LINKS * p
                dve.wait_ge(s_fc1, p + 1)
                nc.vector.tensor_scalar(wrange[:], tiny[:, 2 + K:3 + K], wmax[:], None, ALU.add)
                link(n + 2, nc.vector.tensor_tensor(hid[:], tiny[:, 2:2 + K], small_sb[:, B1:B1 + K], ALU.add))
                fc2 = small_sb[:, FC2:FC2 + K * K].rearrange("p (j k) -> p j k", k=K)
                link(n + 3, nc.vector.scalar_tensor_tensor(
                    out=prod[:], in0=hid[:].unsqueeze(1).to_broadcast([P, K, K]), scalar=0.0, in1=fc2,
                    op0=ALU.max, op1=ALU.mult))
                link(n + 4, nc.vector.tensor_reduce(logit[:], prod[:], AX.X, ALU.add))
                link(n + 5, nc.vector.tensor_tensor(logit_b[:], logit[:], small_sb[:, B2:B2 + K], ALU.add))
                nc.vector.tensor_reduce(nmax[:], logit_b[:], AX.X, ALU.max, negate=True).then_inc(s_logit, 1)
                link(n + 6, nc.vector.reciprocal(wrecip[:], wrange[:]))
                nc.vector.tensor_scalar(wsc[i][:], wrecip[:], WLIMIT, None, ALU.mult)
                nc.vector.tensor_scalar(par[i][:, 0:1], wrange[:], 1.0 / (WLIMIT * XSCALE), None, ALU.mult)

            def softmax(p, i):
                n = LINKS * p
                dve.wait_ge(s_exp, p + 1)
                link(n + 7, nc.vector.tensor_reduce(exsum[:], ex[:], AX.X, ALU.add))
                link(n + 8, nc.vector.reciprocal(rsum[:], exsum[:]))
                link(n + 9, nc.vector.tensor_scalar(att[i][:], ex[:], rsum[:], None, ALU.mult))
                link(n + 10, nc.vector.tensor_tensor(bprod[:], att[i][:], small_sb[:, BIAS:BIAS + K], ALU.mult))
                link(n + 11, nc.vector.tensor_reduce(bsum[:], bprod[:], AX.X, ALU.add))
                nc.vector.tensor_tensor(par[i][:, 1:2], bsum[:], gm[:, 0:1], ALU.add).then_inc(s_par, 1)

            def mixture(p, i):
                for k in range(K):
                    share = dict(out=mix[:], in0=w_sb[:, k, :])
                    if k == 0:
                        last = nc.vector.tensor_scalar(**share, scalar1=att[i][:, 0:1], scalar2=None, op0=ALU.mult)
                    else:
                        last = nc.vector.scalar_tensor_tensor(**share, scalar=att[i][:, k:k + 1], in1=mix[:],
                                                              op0=ALU.mult, op1=ALU.add)
                    last.then_inc(s_part, 1)
                    dve.wait_ge(s_part, K * p + k + 1)
                centre = mix[:, CENTRE * C:(CENTRE + 1) * C]
                nc.vector.scalar_tensor_tensor(out=centre, in0=eye[:], scalar=std[i][:], in1=centre,
                                               op0=ALU.mult, op1=ALU.add).then_inc(s_mix, 1)

            def low_weights(p, i, before):
                dve.wait_ge(s_wh, p + 1)
                if before is not None:
                    dve.wait_ge(w_in[1 - i], W_SEM * before)
                nc.vector.scalar_tensor_tensor(out=wl[:], in0=mix[:], scalar=wsc[i][:], in1=wh[:],
                                               op0=ALU.mult, op1=ALU.subtract).then_inc(s_wl, 1)

            def low_inputs(p, i, before):
                if before is not None:
                    dve.wait_ge(l_in[1 - i], L_SEM * before)
                for half in range(2):
                    dve.wait_ge(s_xh, 2 * p + half + 1)
                    nc.vector.tensor_tensor(inner(xl, half), rows_of(x_sb[i], half),
                                            inner(xh, half), ALU.subtract).then_inc(s_xl, 1)

            def keep_params(p, i, free):
                dve.wait_ge(s_par, p + 1)
                if free:
                    dve.wait_ge(s_res, GROUPS * (p - 1))
                nc.vector.tensor_copy(out_par[i][:], par[i][:]).then_inc(s_outp, 1)

            def copy_high(p, i, m, free):
                if free:
                    dve.wait_ge(s_conv, GROUPS * (p - 1))
                own = halves[m]
                for kind in (LOW, BELOW, RIGHT):
                    last = nc.vector.tensor_copy(mov[i][m][own, kind, :].bitcast(fp32), xh[own, :].bitcast(fp32))
                last.then_inc(s_same, 1)

            def step(p, i, nth, before, free=True, more=True):
                if more:
                    channel_stats(p + 1, 1 - i, nth)
                keep_params(p, i, free)
                if more:
                    channel_moments()
                mixture(p, i)
                low_inputs(p, i, before)
                copy_high(p, i, 0, free)
                low_weights(p, i, before)
                if more:
                    logits(p + 1, 1 - i)
                copy_high(p, i, 1, free)
                if more:
                    softmax(p + 1, 1 - i)

            nc.vector.memset(xh[:].bitcast(fp32), 0.0)
            nc.vector.memset(xl[:].bitcast(fp32), 0.0)
            for i in range(2):
                for m in range(2):
                    last = nc.vector.memset(st_lo[i][m][halves[1 - m], (LO_TAPS - 1) * C:LO_TAPS * C], 0.0)
            last.then_inc(s_zero, 1)
            dve.wait_ge(s_const, 16 * 3)
            nc.vector.tensor_reduce(wpart[:], w_sb[:], AX.XY, ALU.max,
                                    apply_absolute_value=True).then_inc(s_wpart, 1)
            channel_stats(0, 0, 1)
            channel_moments()
            dve.wait_ge(s_wmax, 1)
            logits(0, 0)
            softmax(0, 0)
            step(0, 0, 1, None, free=False)
            step(1, 1, 2, 1, free=False)
            with dve.Fori(1, PAIRS // 2 - 1) as q:
                step(2 * q, 0, q + 1, q)
                step(2 * q + 1, 1, q + 2, q + 1)
            step(PAIRS - 2, 0, PAIRS // 2, PAIRS // 2 - 1)
            step(PAIRS - 1, 1, None, PAIRS // 2, more=False)

        @block.scalar
        def _(act):
            def normalise(p, i):
                act.wait_ge(s_norm, p + 1)
                for half in range(2):
                    v = rows_of(x_sb[i], half)
                    nc.scalar.activation(v, v, ACT.Identity, bias=xof[i][:], scale=xsc[i][:]).then_inc(s_xn, 1)

            def high_weights(p, i, before):
                act.wait_ge(s_mix, p + 1)
                if before is not None:
                    act.wait_ge(w_in[1 - i], W_SEM * before)
                nc.scalar.activation(wh[:], mix[:], ACT.Copy, scale=wsc[i][:]).then_inc(s_wh, 1)

            def high_inputs(p, i, before):
                if before is not None:
                    act.wait_ge(s_same, 2 * p)
                    act.wait_ge(h_in[1 - i], H_SEM * before)
                for half in range(2):
                    act.wait_ge(s_xn, 2 * p + half + 1)
                    nc.scalar.activation(inner(xh, half), rows_of(x_sb[i], half), ACT.Copy).then_inc(s_xh, 1)

            def group_copy(p):
                act.wait_ge(s_gm, p + 1)
                nc.scalar.activation(gm[:], tiny[:, 0:2], ACT.Copy).then_inc(s_gcopy, 1)

            def exponentials(p):
                act.wait_ge(s_logit, p + 1)
                nc.scalar.activation(ex[:], logit_b[:], ACT.Exp, bias=nmax[:]).then_inc(s_exp, 1)

            def results(p, i, t, before):
                if t == 0:
                    act.wait_ge(s_outp, p + 1)
                    if before is not None:
                        act.wait_ge(stored[i], O_SEM * before)
                act.wait_ge(s_conv, GROUPS * p + t + 1)
                nc.scalar.activation(o_sb[i][:, t * GN:(t + 1) * GN], acc[t][:, 0:GN], ACT.Identity,
                                     bias=out_par[i][:, 1:2], scale=out_par[i][:, 0:1]).then_inc(s_res, 1)

            def step(p, i, before, res_before=None, last=True, more=True):
                def out(*banks):
                    if last:
                        for t in banks:
                            results(p - 1, 1 - i, t, res_before)

                out(0)
                if more:
                    group_copy(p + 1)
                high_weights(p, i, before)
                out(1, 2)
                if more:
                    normalise(p + 1, 1 - i)
                out(3)
                if more:
                    exponentials(p + 1)
                out(4, 5)
                if more:
                    high_inputs(p + 1, 1 - i, nth(p, before, i))
                out(6)

            def nth(p, before, i):
                if before is None:
                    return 1
                return before + 1 if i == 0 else before

            act.wait_ge(s_zero, 1)
            group_copy(0)
            normalise(0, 0)
            exponentials(0)
            high_inputs(0, 0, None)
            step(0, 0, None, last=False)
            step(1, 1, 1)
            step(2, 0, 1)
            with act.Fori(1, PAIRS // 2 - 1) as q:
                step(2 * q + 1, 1, q + 1, q)
                step(2 * q + 2, 0, q + 1, q)
            step(PAIRS - 1, 1, PAIRS // 2, PAIRS // 2 - 1, more=False)
            for t in range(GROUPS):
                results(PAIRS - 1, 1, t, PAIRS // 2 - 1)

        @block.tensor
        def _(pe):
            def group_means(p):
                pe.wait_ge(s_mv, p + 1)
                nc.tensor.matmul(tiny[:, 0:2], group[:], mv[:], start=True, stop=True).then_inc(s_gm, 1)

            def image_sums(p):
                pe.wait_ge(s_sums, p + 1)
                nc.tensor.matmul(tiny[:, 2:3 + K], image[:], sums[:], start=True, stop=True).then_inc(s_fc1, 1)

            def convolve(p, i, t, free):
                if free:
                    pe.wait_ge(s_res, GROUPS * (p - 1) + t + 1)
                blocks = [(st_hi, n, LOW, tap // 3, tap % 3) for n, tap in enumerate(TAP_ORDER)]
                blocks += [(st_lo, n, BELOW, 0, n) for n in range(3)]
                blocks += [(st_lo, 3, RIGHT, 2, 0), (st_lo, 4, LOW, 2, 2)]
                for n, (st, slot, kind, kh, kw) in enumerate(blocks):
                    for m in range(2):
                        r0 = t * ROWS + kh
                        last = nc.tensor.matmul(acc[t][halves[m], 0:GN], st[i][m][:, slot * C:(slot + 1) * C],
                                                plane(mov[i][m][:, kind, :])[:, r0:r0 + ROWS, kw:kw + W],
                                                start=n == 0, stop=n == len(blocks) - 1)
                last.then_inc(s_conv, 1)

            def step(p, i, nth, free=True, more=True):
                pe.wait_ge(w_in[i], W_SEM * nth)
                pe.wait_ge(h_in[i], H_SEM * nth)
                pe.wait_ge(l_in[i], L_SEM * nth)
                pe.wait_ge(s_same, 2 * (p + 1))
                for t in range(GROUPS):
                    convolve(p, i, t, free)
                    if more and t == 1:
                        group_means(p + 2)
                    if more and t == 3:
                        image_sums(p + 2)

            pe.wait_ge(s_sel, 5)
            for p in range(2):
                group_means(p)
                image_sums(p)
            step(0, 0, 1, free=False)
            step(1, 1, 1)
            with pe.Fori(1, PAIRS // 2 - 1) as q:
                step(2 * q, 0, q + 1)
                step(2 * q + 1, 1, q + 1)
            step(PAIRS - 2, 0, PAIRS // 2, more=False)
            step(PAIRS - 1, 1, PAIRS // 2, more=False)


def kernel(x, L0_conv_weight, L0_conv_bias, L0_conv_fc1_w, L0_conv_fc1_b, L0_conv_fc2_w, L0_conv_fc2_b):
    import numpy as np
    import concourse.bacc as bacc
    from concourse.bass_utils import run_bass_kernel_spmd

    w = np.asarray(L0_conv_weight).reshape(K, C, C, TAPS)[..., list(TAP_ORDER)]
    arrays = {
        "x": np.ascontiguousarray(x),
        "w_t": np.ascontiguousarray(w.transpose(2, 0, 3, 1).reshape(C, K, TAPS * C)),
        "small": np.ascontiguousarray(np.concatenate([
            np.tile(np.asarray(L0_conv_fc1_w).T, (2, 1)),
            np.tile(np.asarray(L0_conv_bias).T, (2, 1)),
            np.tile(np.asarray(L0_conv_fc1_b)[None], (P, 1)),
            np.tile(np.asarray(L0_conv_fc2_w).reshape(1, K * K), (P, 1)),
            np.tile(np.asarray(L0_conv_fc2_b)[None], (P, 1)),
        ], axis=1)),
    }
    nc = bacc.Bacc("TRN2", target_bir_lowering=False, num_devices=1)
    ins = [nc.dram_tensor(n, a.shape, mybir.dt.from_np(a.dtype), kind="ExternalInput").ap()
           for n, a in arrays.items()]
    out = nc.dram_tensor("out", (B, C, H, W), mybir.dt.float32, kind="ExternalOutput").ap()
    dynamic_conv(nc, *ins, out)
    r = run_bass_kernel_spmd(nc, [arrays], core_ids=[0])
    return r.results[0]["out"]
```

```python
import concourse.bass as bass
from concourse import mybir
from concourse.alu_op_type import AluOpType as ALU
from contextlib import ExitStack

B, C, H, W, K, TAPS = 32, 64, 56, 56, 4, 9
PAIRS = B // 2
P = 2 * C
PIX = H * W
PW = W + 2
PAD = (H + 2) * PW
ROWS = 8
GROUPS = H // ROWS
GN = ROWS * W
TOP = 4 * GN
TAP_ORDER = (0, 1, 2, 6, 8, 3, 4, 5, 7)
CENTRE = TAP_ORDER.index(4)
LO_TAPS = 5
XSCALE = 512.0
WLIMIT = 32000.0
EPS = 1e-5
FC1, BIAS, B1, FC2, B2 = 0, K, 2 * K, 3 * K, 3 * K + K * K
SMALL = B2 + K
W_SEM = 16 * 4
H_SEM = 16 * 4
L_SEM = 16 * 2
O_SEM = 16 * 2
PIECES = ((0, 2), (2, 4), (4, 6), (6, 7))
SPLIT = PAD // 2
TOP_BANKS = 3
EARLY_BANKS, LATE_BANKS = range(2), range(2, GROUPS)
ACT_FIRST = 3
GAP_BANKS = 2
WARM_PRODUCTS = 18


def dynamic_conv(nc, x, w_t, small, out):
    fp32, fp16 = mybir.dt.float32, mybir.dt.float16
    ACT, AX = mybir.ActivationFunctionType, mybir.AxisListType

    x_d = x.rearrange("(p i) c h w -> p (i c) (h w)", i=2)
    out_d = out.rearrange("(p i) c h w -> p (i c) (h w)", i=2)

    ctx = ExitStack()
    with ctx:
        def sb(name, shape, dt=fp32):
            return ctx.enter_context(nc.sbuf_tensor(name, shape, dt))

        def sem(name):
            return ctx.enter_context(nc.semaphore(name))

        x_sb = [sb(f"x{i}", [P, PIX]) for i in range(2)]
        o_sb = [sb(f"o{i}", [P, PIX]) for i in range(2)]
        xh = sb("xh", [P, PAD], fp16)
        xl = sb("xl", [P, PAD], fp16)
        LOW, BELOW, RIGHT = range(3)
        mov = [[sb(f"mov{i}{m}", [P, 3, PAD], fp16) for m in range(2)] for i in range(2)]
        w_sb = sb("w_sb", [P, K, TAPS * C])
        mix = sb("mix", [P, TAPS * C])
        wh = sb("wh", [P, TAPS * C], fp16)
        wl = sb("wl", [P, TAPS * C], fp16)
        st_hi = [[sb(f"st_hi{i}{m}", [P, TAPS * C], fp16) for m in range(2)] for i in range(2)]
        st_lo = [[sb(f"st_lo{i}{m}", [P, LO_TAPS * C], fp16) for m in range(2)] for i in range(2)]
        small_sb = sb("small_sb", [P, SMALL])
        group = sb("group", [P, P])
        image = sb("image", [P, P])
        eye = sb("eye", [P, C])
        CONSTS = (EPS, -0.5, 1.5, XSCALE, -XSCALE)
        consts = sb("consts", [P, len(CONSTS)])
        warm = sb("warm", [P, 1])
        wpart = sb("wpart", [P, 1])
        wmax = sb("wmax", [P, 1])
        stats = sb("stats", [P, GROUPS, 6])
        mv = sb("mv", [P, 2])
        dev = sb("dev", [P, 1])
        dev2 = sb("dev2", [P, 1])
        gvar = sb("gvar", [P, 1])
        pooled = sb("pooled", [P, 1])
        noff = sb("noff", [P, 1])
        var = sb("var", [P, 1])
        root = sb("root", [P, 1])
        newton = sb("newton", [P, 4])
        rstd = sb("rstd", [P, 1])
        sums = sb("sums", [P, K + 1])
        hid = sb("hid", [P, K])
        prod = sb("prod", [P, K, K])
        logit = sb("logit", [P, K])
        logit_b = sb("logit_b", [P, K])
        nmax = sb("nmax", [P, 1])
        ex = sb("ex", [P, K])
        exsum = sb("exsum", [P, 1])
        rsum = sb("rsum", [P, 1])
        bprod = sb("bprod", [P, K])
        bsum = sb("bsum", [P, 1])
        wrange = sb("wrange", [P, 1])
        wrecip = sb("wrecip", [P, 1])
        gm = [sb(f"gm{i}", [P, 2]) for i in range(2)]
        att = [sb(f"att{i}", [P, K]) for i in range(2)]
        std = [sb(f"std{i}", [P, 1]) for i in range(2)]
        xsc = [sb(f"xsc{i}", [P, 1]) for i in range(2)]
        xof = [sb(f"xof{i}", [P, 1]) for i in range(2)]
        wsc = [sb(f"wsc{i}", [P, 1]) for i in range(2)]
        par = [sb(f"par{i}", [P, 2]) for i in range(2)]
        out_par = [sb(f"out_par{i}", [P, 2]) for i in range(2)]

        acc = [ctx.enter_context(nc.psum_tensor(f"acc{t}", [P, 512], fp32)) for t in range(GROUPS)]
        tiny = ctx.enter_context(nc.psum_tensor("tiny", [P, 512], fp32))

        s_small = sem("s_small")
        s_weights = sem("s_weights")
        s_sel = sem("s_sel")
        s_warm = sem("s_warm")
        s_zero = sem("s_zero")
        s_wpart = sem("s_wpart")
        s_wmax = sem("s_wmax")
        x_top = [sem(f"x_top{i}") for i in range(2)]
        x_bot = [sem(f"x_bot{i}") for i in range(2)]
        x_piece = [sem(f"x_piece{n}") for n in range(2)]
        dch = sem("dch")
        s_stats = sem("s_stats")
        s_mv = sem("s_mv")
        s_gm = sem("s_gm")
        s_gcopy = sem("s_gcopy")
        pch = sem("pch")
        gch = sem("gch")
        s_var = sem("s_var")
        s_root = sem("s_root")
        s_norm = sem("s_norm")
        s_sums = sem("s_sums")
        s_fc1 = sem("s_fc1")
        s_logit = sem("s_logit")
        s_exp = sem("s_exp")
        s_par = sem("s_par")
        s_part = sem("s_part")
        s_mix = sem("s_mix")
        s_wh = sem("s_wh")
        s_wl = sem("s_wl")
        s_xn = sem("s_xn")
        s_xh = sem("s_xh")
        s_xl = sem("s_xl")
        s_same = sem("s_same")
        act_same = sem("act_same")
        pool_same = sem("pool_same")
        s_own = sem("s_own")
        w_in = [sem(f"w_in{i}") for i in range(2)]
        h_in = [sem(f"h_in{i}") for i in range(2)]
        l_in = [sem(f"l_in{i}") for i in range(2)]
        h_top = sem("h_top")
        l_top = sem("l_top")
        s_conv = sem("s_conv")
        s_outp = sem("s_outp")
        s_res = sem("s_res")
        stored = [sem(f"stored{i}") for i in range(2)]

        def const(value):
            n = CONSTS.index(value)
            return consts[:, n:n + 1]

        def plane(t):
            return t.rearrange("p (r c) -> p r c", c=PW)

        def inner(t, half):
            r0 = half * H // 2
            return plane(t)[:, 1 + r0:1 + r0 + H // 2, 1:1 + W]

        def rows_of(t, half):
            return t.rearrange("p (r c) -> p r c", c=W)[:, half * H // 2:(half + 1) * H // 2, :]

        halves = (slice(0, C), slice(C, P))

        block = ctx.enter_context(nc.Block())

        @block.sync
        def _(sp):
            def load_top(p, i):
                sp.dma_start(x_sb[i][:, 0:TOP], x_d[p, :, 0:TOP]).then_inc(x_top[i], 16)

            def load_bottom(p, i):
                sp.dma_start(x_sb[i][:, TOP:PIX], x_d[p, :, TOP:PIX]).then_inc(x_bot[i], 16)

            def load(p, i):
                load_top(p, i)
                load_bottom(p, i)

            def spread_high_weights(p, i):
                sp.wait_ge(s_wh, p + 1)
                for m in range(2):
                    own, other = halves[m], halves[1 - m]
                    sp.dma_start(st_hi[i][m][other, :], wh[own, :]).then_inc(w_in[i], 16)

            def spread_low_weights(p, i):
                sp.wait_ge(s_wl, p + 1)
                for m in range(2):
                    own, other = halves[m], halves[1 - m]
                    sp.dma_start(st_lo[i][m][other, 0:(LO_TAPS - 1) * C],
                                 wl[own, LO_TAPS * C:TAPS * C]).then_inc(w_in[i], 16)

            def send_high(i, start, stop, signal):
                for kind, shift in ((BELOW, PW), (RIGHT, 1)):
                    for m in range(2):
                        own, other = halves[m], halves[1 - m]
                        first = max(start - shift, 0)
                        sp.dma_start(mov[i][m][other, kind, first:stop - shift],
                                     xh[own, first + shift:stop]).then_inc(signal, 16)

            def send_low(i, start, stop, signal):
                for m in range(2):
                    own, other = halves[m], halves[1 - m]
                    sp.dma_start(mov[i][m][other, LOW, start:stop], xl[own, start:stop]).then_inc(signal, 16)

            def spread_high(p, i, free):
                sp.wait_ge(s_xh, 2 * (p + 1))
                if free:
                    sp.wait_ge(s_conv, GROUPS * (p - 1))
                send_high(i, 0, PAD, h_in[i])

            def spread_low(p, i):
                sp.wait_ge(s_xl, 2 * (p + 1))
                send_low(i, 0, PAD, l_in[i])

            def store_top(p, i):
                sp.wait_ge(s_res, GROUPS * p + TOP // GN)
                sp.dma_start(out_d[p, :, 0:TOP], o_sb[i][:, 0:TOP]).then_inc(stored[i], 16)

            def store_bottom(p, i):
                sp.wait_ge(s_res, GROUPS * (p + 1))
                sp.dma_start(out_d[p, :, TOP:PIX], o_sb[i][:, TOP:PIX]).then_inc(stored[i], 16)

            def step(p, i, more):
                spread_high(p, i, True)
                spread_high_weights(p, i)
                spread_low_weights(p, i)
                spread_low(p, i)
                if more:
                    load(p + 2, i)
                store_top(p - 1, 1 - i)
                store_bottom(p - 1, 1 - i)

            for (first, last), signal in zip(PIECES, (x_piece[0], x_top[0], x_piece[1], x_bot[0])):
                pixels = slice(first * GN, last * GN)
                sp.dma_start(x_sb[0][:, pixels], x_d[0, :, pixels]).then_inc(signal, 16)
            sp.dma_start(small_sb[:], small).then_inc(s_small, 16)
            for half in halves:
                sp.dma_start(w_sb[half, :, :], w_t).then_inc(s_weights, 16)
            load(1, 1)
            sp.wait_ge(s_xh, 1)
            send_high(0, 0, SPLIT, h_top)
            spread_high_weights(0, 0)
            spread_low_weights(0, 0)
            sp.wait_ge(s_xl, 1)
            send_low(0, 0, SPLIT, l_top)
            sp.wait_ge(s_xh, 2)
            send_high(0, SPLIT, PAD, h_in[0])
            sp.wait_ge(s_xl, 2)
            send_low(0, SPLIT, PAD, l_in[0])
            load(2, 0)
            spread_high(1, 1, False)
            spread_high_weights(1, 1)
            spread_low_weights(1, 1)
            spread_low(1, 1)
            load(3, 1)
            store_top(0, 0)
            store_bottom(0, 0)
            with sp.Fori(1, PAIRS // 2 - 1) as q:
                step(2 * q, 0, True)
                step(2 * q + 1, 1, True)
            step(PAIRS - 2, 0, False)
            step(PAIRS - 1, 1, False)
            store_top(PAIRS - 1, 1)
            for t in range(TOP // GN, GROUPS):
                sp.wait_ge(s_res, GROUPS * (PAIRS - 1) + t + 1)
                bank = slice(t * GN, (t + 1) * GN)
                sp.dma_start(out_d[PAIRS - 1, :, bank], o_sb[1][:, bank]).then_inc(stored[1], 16)
            sp.wait_ge(stored[0], O_SEM * PAIRS // 2)
            sp.wait_ge(stored[1], O_SEM * PAIRS // 2 + 16 * (GROUPS - 1 - TOP // GN))

        @block.gpsimd
        def _(pool):
            nc.gpsimd.memset(group[:], 0.5)
            nc.gpsimd.memset(image[:], 1.0)
            nc.gpsimd.memset(eye[:], 0.0)
            for n, value in enumerate(CONSTS):
                last = nc.gpsimd.memset(consts[:, n:n + 1], value)
            last.then_inc(s_sel, 1)
            pool.wait_ge(s_sel, 1)
            pairs_of = group[:].rearrange("k (g j) -> k g j", j=2)
            nc.gpsimd.affine_select(out=pairs_of, in_=pairs_of, compare_op=ALU.is_ge, fill=0.0, base=0,
                                    pattern=[[-2, P // 2], [0, 2]], channel_multiplier=1).then_inc(s_sel, 1)
            pool.wait_ge(s_sel, 2)
            nc.gpsimd.affine_select(out=pairs_of, in_=pairs_of, compare_op=ALU.is_ge, fill=0.0, base=1,
                                    pattern=[[2, P // 2], [0, 2]], channel_multiplier=-1).then_inc(s_sel, 1)
            low = image[:, 0:C]
            nc.gpsimd.affine_select(out=low, in_=low, compare_op=ALU.is_ge, fill=0.0, base=C - 1,
                                    pattern=[[0, C]], channel_multiplier=-1)
            high = image[:, C:P]
            nc.gpsimd.affine_select(out=high, in_=high, compare_op=ALU.is_ge, fill=0.0, base=-C,
                                    pattern=[[0, C]], channel_multiplier=1)
            nc.gpsimd.affine_select(out=eye[:], in_=eye[:], compare_op=ALU.not_equal, fill=1.0, base=0,
                                    pattern=[[-1, C]], channel_multiplier=1).then_inc(s_sel, 1)
            pool.wait_ge(s_sel, 4)
            nc.gpsimd.affine_select(out=eye[:], in_=eye[:], compare_op=ALU.not_equal, fill=1.0, base=-C,
                                    pattern=[[-1, C]], channel_multiplier=1).then_inc(s_sel, 1)
            nc.gpsimd.memset(xh[:].bitcast(fp32), 0.0)
            nc.gpsimd.memset(xl[:].bitcast(fp32), 0.0).then_inc(s_zero, 1)

            CHAIN = 12
            BY_DVE = 2

            def link(n, ins):
                ins.then_inc(pch, 1)
                pool.wait_ge(pch, n)

            def group_stats(p, i, before):
                n = CHAIN * before
                tt = nc.gpsimd.tensor_tensor
                pool.wait_ge(s_gcopy, before + 1)
                link(n + 1, tt(dev[:], mv[:, 0:1], gm[i][:, 0:1], ALU.subtract))
                link(n + 2, tt(dev2[:], dev[:], dev[:], ALU.mult))
                link(n + 3, tt(gvar[:], dev2[:], gm[i][:, 1:2], ALU.add))
                link(n + 4, tt(var[:], gvar[:], const(EPS), ALU.add))
                link(n + 5, tt(root[:], var[:], const(-0.5), ALU.pow))
                link(n + 6, tt(newton[:, 0:1], root[:], root[:], ALU.mult))
                link(n + 7, tt(newton[:, 1:2], newton[:, 0:1], var[:], ALU.mult))
                link(n + 8, tt(newton[:, 2:3], newton[:, 1:2], const(-0.5), ALU.mult))
                link(n + 9, tt(newton[:, 3:4], newton[:, 2:3], const(1.5), ALU.add))
                link(n + 10, tt(rstd[:], root[:], newton[:, 3:4], ALU.mult))
                tt(std[i][:], var[:], rstd[:], ALU.mult)
                tt(sums[:, K:K + 1], var[:], rstd[:], ALU.mult)
                tt(xsc[i][:], rstd[:], const(XSCALE), ALU.mult)
                link(n + 11, tt(pooled[:], dev[:], rstd[:], ALU.mult))
                tt(sums[:, 0:K], small_sb[:, FC1:FC1 + K], pooled[:].to_broadcast([P, K]),
                   ALU.mult).then_inc(s_sums, 1)
                link(n + 12, tt(noff[:], gm[i][:, 0:1], const(-XSCALE), ALU.mult))
                tt(xof[i][:], noff[:], rstd[:], ALU.mult).then_inc(s_norm, 1)

            def take_root(p):
                pool.wait_ge(s_var, p)
                nc.gpsimd.tensor_tensor(root[:], var[:], const(-0.5), ALU.pow).then_inc(s_root, 1)

            def copy_high(n, i, kind, part):
                for m in range(2):
                    own = halves[m]
                    nc.gpsimd.tensor_copy(mov[i][m][own, kind, part].bitcast(fp32),
                                          xh[own, part].bitcast(fp32)).then_inc(pool_same, 1)
                    pool.wait_ge(pool_same, n + m + 1)

            pool.wait_ge(s_small, 16)
            group_stats(0, 0, 0)
            pool.wait_ge(s_wpart, 1)
            nc.gpsimd.partition_all_reduce(wmax[:], wpart[:], P, bass.bass_isa.ReduceOp.max).then_inc(s_wmax, 1)
            pool.wait_ge(s_xh, 1)
            copy_high(0, 0, BELOW, slice(0, SPLIT))
            copy_high(2, 0, RIGHT, slice(0, SPLIT))
            take_root(1)
            pool.wait_ge(s_xh, 4)
            copy_high(4, 1, RIGHT, slice(0, PAD))
            take_root(2)
            group_stats(3, 1, 1)
            with pool.Fori(2, PAIRS // 2) as q:
                group_stats(2 * q, 0, 2 * q - BY_DVE)
                group_stats(2 * q + 1, 1, 2 * q + 1 - BY_DVE)

        @block.vector
        def _(dve):
            LINKS = 11
            GROUP_LINKS = 7

            def link(n, ins):
                ins.then_inc(dch, 1)
                dve.wait_ge(dch, n)

            def channel_stats(i, nth, banks=range(GROUPS)):
                for t in banks:
                    if nth is not None and t == 0:
                        dve.wait_ge(x_top[i], 16 * nth)
                    if nth is not None and t == TOP // GN:
                        dve.wait_ge(x_bot[i], 16 * nth)
                    last = nc.vector.bn_stats(stats[:, t, :], x_sb[i][:, t * GN:(t + 1) * GN])
                if t == GROUPS - 1:
                    last.then_inc(s_stats, 1)

            def channel_moments():
                nc.vector.bn_aggr(mv[:], stats[:]).then_inc(s_mv, 1)

            def group_stats(p, i):
                n = GROUP_LINKS * (p - 1)
                dve.wait_ge(s_gm, p + 1)

                def glink(k, ins):
                    ins.then_inc(gch, 1)
                    dve.wait_ge(gch, n + k)

                glink(1, nc.vector.tensor_copy(gm[i][:], tiny[:, 0:2]))
                glink(2, nc.vector.tensor_tensor(dev[:], mv[:, 0:1], gm[i][:, 0:1], ALU.subtract))
                glink(3, nc.vector.scalar_tensor_tensor(out=gvar[:], in0=dev[:], scalar=dev[:], in1=gm[i][:, 1:2],
                                                        op0=ALU.mult, op1=ALU.add))
                nc.vector.tensor_scalar(var[:], gvar[:], EPS, None, ALU.add).then_inc(s_var, 1)
                dve.wait_ge(s_root, p)
                glink(4, nc.vector.scalar_tensor_tensor(out=newton[:, 0:1], in0=root[:], scalar=root[:], in1=var[:],
                                                        op0=ALU.mult, op1=ALU.mult))
                glink(5, nc.vector.tensor_scalar(newton[:, 1:2], newton[:, 0:1], -0.5, 1.5, ALU.mult, ALU.add))
                glink(6, nc.vector.tensor_tensor(rstd[:], root[:], newton[:, 1:2], ALU.mult))
                nc.vector.tensor_tensor(sums[:, K:K + 1], var[:], rstd[:], ALU.mult)
                glink(7, nc.vector.tensor_tensor(pooled[:], dev[:], rstd[:], ALU.mult))
                nc.vector.tensor_scalar(sums[:, 0:K], small_sb[:, FC1:FC1 + K], pooled[:], None,
                                        ALU.mult).then_inc(s_sums, 1)
                nc.vector.tensor_scalar(xsc[i][:], rstd[:], XSCALE, None, ALU.mult)
                nc.vector.tensor_scalar(xof[i][:], gm[i][:, 0:1], -XSCALE, rstd[:], ALU.mult,
                                        ALU.mult).then_inc(s_norm, 1)
                nc.vector.tensor_tensor(std[i][:], var[:], rstd[:], ALU.mult)

            def logits(p, i, first=False):
                n = LINKS * p
                dve.wait_ge(s_fc1, p + 1)
                link(n + 1, nc.vector.tensor_tensor(hid[:], tiny[:, 2:2 + K], small_sb[:, B1:B1 + K], ALU.add))
                fc2 = small_sb[:, FC2:FC2 + K * K].rearrange("p (j k) -> p j k", k=K)
                link(n + 2, nc.vector.scalar_tensor_tensor(
                    out=prod[:], in0=hid[:].unsqueeze(1).to_broadcast([P, K, K]), scalar=0.0, in1=fc2,
                    op0=ALU.max, op1=ALU.mult))
                link(n + 3, nc.vector.tensor_reduce(logit[:], prod[:], AX.X, ALU.add))
                link(n + 4, nc.vector.tensor_tensor(logit_b[:], logit[:], small_sb[:, B2:B2 + K], ALU.add))
                nc.vector.tensor_reduce(nmax[:], logit_b[:], AX.X, ALU.max, negate=True).then_inc(s_logit, 1)
                if first:
                    dve.wait_ge(s_wmax, 1)
                link(n + 5, nc.vector.tensor_scalar(wrange[:], tiny[:, 2 + K:3 + K], wmax[:], None, ALU.add))
                link(n + 6, nc.vector.reciprocal(wrecip[:], wrange[:]))
                nc.vector.tensor_scalar(wsc[i][:], wrecip[:], WLIMIT, None, ALU.mult)
                nc.vector.tensor_scalar(par[i][:, 0:1], wrange[:], 1.0 / (WLIMIT * XSCALE), None, ALU.mult)

            def softmax(p, i):
                n = LINKS * p
                dve.wait_ge(s_exp, p + 1)
                link(n + 7, nc.vector.tensor_reduce(exsum[:], ex[:], AX.X, ALU.add))
                link(n + 8, nc.vector.reciprocal(rsum[:], exsum[:]))
                link(n + 9, nc.vector.tensor_scalar(att[i][:], ex[:], rsum[:], None, ALU.mult))
                link(n + 10, nc.vector.tensor_tensor(bprod[:], att[i][:], small_sb[:, BIAS:BIAS + K], ALU.mult))
                link(n + 11, nc.vector.tensor_reduce(bsum[:], bprod[:], AX.X, ALU.add))
                nc.vector.tensor_tensor(par[i][:, 1:2], bsum[:], gm[i][:, 0:1], ALU.add).then_inc(s_par, 1)

            def mixture(p, i):
                for k in range(K):
                    share = dict(out=mix[:], in0=w_sb[:, k, :])
                    if k == 0:
                        last = nc.vector.tensor_scalar(**share, scalar1=att[i][:, 0:1], scalar2=None, op0=ALU.mult)
                    else:
                        last = nc.vector.scalar_tensor_tensor(**share, scalar=att[i][:, k:k + 1], in1=mix[:],
                                                              op0=ALU.mult, op1=ALU.add)
                    last.then_inc(s_part, 1)
                    dve.wait_ge(s_part, K * p + k + 1)
                centre = mix[:, CENTRE * C:(CENTRE + 1) * C]
                nc.vector.scalar_tensor_tensor(out=centre, in0=eye[:], scalar=std[i][:], in1=centre,
                                               op0=ALU.mult, op1=ALU.add).then_inc(s_mix, 1)

            def low_weights(p, i, before):
                dve.wait_ge(s_wh, p + 1)
                if before is not None:
                    dve.wait_ge(w_in[1 - i], W_SEM * before)
                nc.vector.scalar_tensor_tensor(out=wl[:], in0=mix[:], scalar=wsc[i][:], in1=wh[:],
                                               op0=ALU.mult, op1=ALU.subtract).then_inc(s_wl, 1)

            def own_weights(p, i, free):
                dve.wait_ge(s_wl, p + 1)
                if free:
                    dve.wait_ge(s_conv, GROUPS * (p - 1))
                for m in range(2):
                    own = halves[m]
                    for st, source, columns in ((st_hi, wh, TAPS * C), (st_lo, wl, LO_TAPS * C)):
                        last = nc.vector.tensor_copy(st[i][m][own, 0:columns].bitcast(fp32),
                                                     source[own, 0:columns].bitcast(fp32))
                last.then_inc(s_own, 1)

            def low_inputs(p, i, before, parts=range(2)):
                if before is not None:
                    dve.wait_ge(l_in[1 - i], L_SEM * before)
                for half in parts:
                    dve.wait_ge(s_xn, 2 * p + half + 1)
                    dve.wait_ge(s_xh, 2 * p + half + 1)
                    nc.vector.tensor_tensor(inner(xl, half), rows_of(x_sb[i], half),
                                            inner(xh, half), ALU.subtract).then_inc(s_xl, 1)

            def keep_params(p, i, free):
                dve.wait_ge(s_par, p + 1)
                if free:
                    dve.wait_ge(s_res, GROUPS * (p - 1))
                nc.vector.tensor_copy(out_par[i][:], par[i][:]).then_inc(s_outp, 1)

            def copy_high(p, i, kind, free, part=slice(0, PAD), amount=1, images=range(2)):
                if free:
                    dve.wait_ge(s_conv, GROUPS * (p - 1))
                for m in images:
                    own = halves[m]
                    last = nc.vector.tensor_copy(mov[i][m][own, kind, part].bitcast(fp32),
                                                 xh[own, part].bitcast(fp32))
                last.then_inc(s_same, amount)

            def step(p, i, before, nth=None, free=True, more=True):
                if more:
                    dve.wait_ge(s_stats, p + 2)
                keep_params(p, i, free)
                if more:
                    channel_moments()
                mixture(p, i)
                low_inputs(p, i, before, (0,))
                low_weights(p, i, before)
                low_inputs(p, i, before, (1,))
                own_weights(p, i, free)
                copy_high(p, i, BELOW, free)
                copy_high(p, i, RIGHT, free)
                copy_high(p, i, LOW, free, images=(0,))
                if more:
                    logits(p + 1, 1 - i)
                    softmax(p + 1, 1 - i)
                if nth is not None:
                    channel_stats(i, nth)

            nc.vector.memset(warm[:], 0.0).then_inc(s_warm, 1)
            for i in range(2):
                for m in range(2):
                    last = nc.vector.memset(st_lo[i][m][halves[1 - m], (LO_TAPS - 1) * C:LO_TAPS * C], 0.0)
            last.then_inc(s_zero, 1)
            for (first, last), signal in zip(PIECES, (x_piece[0], x_top[0], x_piece[1], x_bot[0])):
                dve.wait_ge(signal, 16)
                channel_stats(0, None, range(first, last))
            dve.wait_ge(s_stats, 1)
            channel_moments()
            dve.wait_ge(s_small, 16)
            dve.wait_ge(s_weights, 16 * 2)
            nc.vector.tensor_reduce(wpart[:], w_sb[:], AX.XY, ALU.max,
                                    apply_absolute_value=True).then_inc(s_wpart, 1)
            dve.wait_ge(s_mv, 1)
            channel_stats(1, 1, EARLY_BANKS)
            logits(0, 0, first=True)
            softmax(0, 0)
            mixture(0, 0)
            low_inputs(0, 0, None, (0,))
            low_weights(0, 0, None)
            own_weights(0, 0, False)
            channel_stats(1, 1, LATE_BANKS)
            dve.wait_ge(s_stats, 2)
            channel_moments()
            low_inputs(0, 0, None, (1,))
            group_stats(1, 1)
            keep_params(0, 0, False)
            logits(1, 1)
            copy_high(0, 0, BELOW, False, slice(SPLIT, PAD), amount=3)
            softmax(1, 1)
            keep_params(1, 1, False)
            mixture(1, 1)
            dve.wait_ge(l_top, L_SEM)
            low_inputs(1, 1, 1, (0,))
            low_weights(1, 1, 1)
            low_inputs(1, 1, 1, (1,))
            copy_high(1, 1, BELOW, False, amount=3)
            channel_stats(0, 2)
            dve.wait_ge(s_stats, 3)
            channel_moments()
            own_weights(1, 1, False)
            group_stats(2, 0)
            channel_stats(1, 2, range(GAP_BANKS))
            logits(2, 0)
            softmax(2, 0)
            channel_stats(1, 2, range(GAP_BANKS, GROUPS))
            with dve.Fori(1, PAIRS // 2 - 1) as q:
                step(2 * q, 0, q, q + 2)
                step(2 * q + 1, 1, q + 1, q + 2)
            step(PAIRS - 2, 0, PAIRS // 2 - 1)
            step(PAIRS - 1, 1, PAIRS // 2, more=False)

        @block.scalar
        def _(act):
            def normalise(p, i, parts=range(2)):
                act.wait_ge(s_norm, p + 1)
                for half in parts:
                    v = rows_of(x_sb[i], half)
                    nc.scalar.activation(v, v, ACT.Identity, bias=xof[i][:], scale=xsc[i][:]).then_inc(s_xn, 1)

            def high_weights(p, i, before):
                act.wait_ge(s_mix, p + 1)
                if before is not None:
                    act.wait_ge(s_own, p)
                    act.wait_ge(w_in[1 - i], W_SEM * before)
                nc.scalar.activation(wh[:], mix[:], ACT.Copy, scale=wsc[i][:]).then_inc(s_wh, 1)

            def high_inputs(p, i, before):
                if before is not None:
                    act.wait_ge(s_same, 3 * p)
                    act.wait_ge(act_same, p + ACT_FIRST - 1)
                    act.wait_ge(h_in[1 - i], H_SEM * before)
                for half in range(2):
                    act.wait_ge(s_xn, 2 * p + half + 1)
                    nc.scalar.activation(inner(xh, half), rows_of(x_sb[i], half), ACT.Copy).then_inc(s_xh, 1)

            def high_from_x(i, half):
                act.wait_ge(s_norm, 1)
                nc.scalar.activation(inner(xh, half), rows_of(x_sb[i], half), ACT.Identity,
                                     bias=xof[i][:], scale=xsc[i][:]).then_inc(s_xh, 1)

            def copy_high(p, i, kind, part=slice(0, PAD), images=range(2)):
                act.wait_ge(s_xh, 2 * (p + 1))
                for m in images:
                    own = halves[m]
                    last = nc.scalar.activation(mov[i][m][own, kind, part], xh[own, part], ACT.Copy)
                last.then_inc(act_same, 1)

            def group_copy(p, i):
                act.wait_ge(s_gm, p + 1)
                nc.scalar.activation(gm[i][:], tiny[:, 0:2], ACT.Copy).then_inc(s_gcopy, 1)

            def exponentials(p):
                act.wait_ge(s_logit, p + 1)
                nc.scalar.activation(ex[:], logit_b[:], ACT.Exp, bias=nmax[:]).then_inc(s_exp, 1)

            def results(p, i, t, before):
                if t == 0:
                    act.wait_ge(s_outp, p + 1)
                    if before is not None:
                        act.wait_ge(stored[i], O_SEM * before)
                act.wait_ge(s_conv, GROUPS * p + t + 1)
                nc.scalar.activation(o_sb[i][:, t * GN:(t + 1) * GN], acc[t][:, 0:GN], ACT.Identity,
                                     bias=out_par[i][:, 1:2], scale=out_par[i][:, 0:1]).then_inc(s_res, 1)

            def step(p, i, before, res_before=None, more=True):
                def out(*banks):
                    for t in banks:
                        results(p - 1, 1 - i, t, res_before)

                out(0)
                if more:
                    group_copy(p + 1, 1 - i)
                high_weights(p, i, before)
                copy_high(p, i, LOW, images=(1,))
                out(1, 2)
                if more:
                    normalise(p + 1, 1 - i)
                out(3)
                if more:
                    exponentials(p + 1)
                out(4, 5)
                if more:
                    high_inputs(p + 1, 1 - i, before + 1 if i == 0 else before)
                out(6)

            act.wait_ge(s_warm, 1)
            nc.scalar.activation(warm[:], warm[:], ACT.Exp)
            act.wait_ge(s_zero, 2)
            group_copy(0, 0)
            high_from_x(0, 0)
            exponentials(0)
            normalise(0, 0, (0,))
            high_from_x(0, 1)
            act.wait_ge(s_xh, 2)
            normalise(0, 0, (1,))
            high_weights(0, 0, None)
            copy_high(0, 0, LOW, slice(0, SPLIT))
            copy_high(0, 0, RIGHT, slice(SPLIT, PAD))
            copy_high(0, 0, LOW, slice(SPLIT, PAD))
            normalise(1, 1, (0,))
            exponentials(1)
            normalise(1, 1, (1,))
            act.wait_ge(pool_same, 4)
            act.wait_ge(h_top, H_SEM)
            high_inputs(1, 1, 1)
            high_weights(1, 1, 1)
            results(0, 0, 0, None)
            copy_high(1, 1, LOW)
            for t in range(1, GROUPS):
                results(0, 0, t, None)
            normalise(2, 0, (0,))
            exponentials(2)
            normalise(2, 0, (1,))
            act.wait_ge(pool_same, 6)
            high_inputs(2, 0, 1)
            step(2, 0, 1)
            with act.Fori(1, PAIRS // 2 - 1) as q:
                step(2 * q + 1, 1, q + 1, q)
                step(2 * q + 2, 0, q + 1, q)
            step(PAIRS - 1, 1, PAIRS // 2, PAIRS // 2 - 1, more=False)
            for t in range(GROUPS):
                results(PAIRS - 1, 1, t, PAIRS // 2 - 1)

        @block.tensor
        def _(pe):
            def group_means(p):
                pe.wait_ge(s_mv, p + 1)
                nc.tensor.matmul(tiny[:, 0:2], group[:], mv[:], start=True, stop=True).then_inc(s_gm, 1)

            def image_sums(p):
                pe.wait_ge(s_sums, p + 1)
                nc.tensor.matmul(tiny[:, 2:3 + K], image[:], sums[:], start=True, stop=True).then_inc(s_fc1, 1)

            def kind_ready(p, i, nth):
                def wait_for(kind):
                    pe.wait_ge(s_same, 3 * p + (BELOW, RIGHT, LOW).index(kind) + 1)
                    if kind == LOW:
                        pe.wait_ge(act_same, p + ACT_FIRST)
                        pe.wait_ge(l_in[i], L_SEM * nth)
                return wait_for

            def upper_ready(kind):
                if kind == LOW:
                    pe.wait_ge(act_same, 1)
                    pe.wait_ge(l_top, L_SEM)
                else:
                    pe.wait_ge(pool_same, 2 if kind == BELOW else 4)

            def convolve(p, i, t, free, wait_for):
                if free:
                    pe.wait_ge(s_res, GROUPS * (p - 1) + t + 1)
                blocks = [(st_lo, n, BELOW, 0, n) for n in (1, 0, 2)]
                blocks += [(st_lo, 3, RIGHT, 2, 0), (st_lo, 4, LOW, 2, 2)]
                blocks += [(st_hi, n, LOW, tap // 3, tap % 3) for n, tap in enumerate(TAP_ORDER)]
                for n, (st, slot, kind, kh, kw) in enumerate(blocks):
                    if t == 0 and kind != blocks[n - 1][2]:
                        wait_for(kind)
                    top = 1 if t == 0 and kh == 0 and kind != BELOW else 0
                    bottom = ROWS - 1 if t == GROUPS - 1 and kh == 2 else ROWS
                    left = 1 if kw == 0 and kind != RIGHT else 0
                    right = W - 1 if kw == 2 else W
                    r0 = t * ROWS + kh
                    for m in range(2):
                        pixels = acc[t][halves[m], 0:GN].rearrange("p (r c) -> p r c", c=W)
                        window = plane(mov[i][m][:, kind, :])[:, r0 + top:r0 + bottom, kw + left:kw + right]
                        last = nc.tensor.matmul(pixels[:, top:bottom, left:right],
                                                st[i][m][:, slot * C:(slot + 1) * C], window,
                                                start=n == 0, stop=n == len(blocks) - 1)
                last.then_inc(s_conv, 1)

            def step(p, i, nth, free=True, visits=((2, group_means, 2), (4, image_sums, 2))):
                pe.wait_ge(s_own, p + 1)
                pe.wait_ge(w_in[i], W_SEM * nth)
                pe.wait_ge(h_in[i], H_SEM * nth)
                for t in range(GROUPS):
                    convolve(p, i, t, free, kind_ready(p, i, nth))
                    for bank, sums_of, ahead in visits:
                        if t == bank:
                            sums_of(p + ahead)

            pe.wait_ge(s_sel, 5)
            group_means(0)
            image_sums(0)
            pe.wait_ge(s_wl, 1)
            for _ in range(WARM_PRODUCTS):
                nc.tensor.matmul(acc[GROUPS - 1][:, 0:2 * P], group[:].bitcast(fp16)[:, 0:P],
                                 group[:].bitcast(fp16), start=True, stop=True)
            group_means(1)
            pe.wait_ge(s_own, 1)
            pe.wait_ge(w_in[0], W_SEM)
            pe.wait_ge(h_top, H_SEM)
            for t in range(TOP_BANKS):
                convolve(0, 0, t, False, upper_ready)
                if t == 0:
                    image_sums(1)
            pe.wait_ge(h_in[0], H_SEM)
            pe.wait_ge(l_in[0], L_SEM)
            pe.wait_ge(s_same, 3)
            pe.wait_ge(act_same, ACT_FIRST)
            for t in range(TOP_BANKS, GROUPS):
                convolve(0, 0, t, False, None)
            group_means(2)
            pe.wait_ge(pool_same, 6)
            step(1, 1, 1, visits=((0, image_sums, 1), (3, group_means, 2), (5, image_sums, 2)))
            with pe.Fori(1, PAIRS // 2 - 1) as q:
                step(2 * q, 0, q + 1)
                step(2 * q + 1, 1, q + 1)
            step(PAIRS - 2, 0, PAIRS // 2, visits=())
            step(PAIRS - 1, 1, PAIRS // 2, visits=())


def kernel(x, L0_conv_weight, L0_conv_bias, L0_conv_fc1_w, L0_conv_fc1_b, L0_conv_fc2_w, L0_conv_fc2_b):
    import numpy as np
    import concourse.bacc as bacc
    from concourse.bass_utils import run_bass_kernel_spmd

    w = np.asarray(L0_conv_weight).reshape(K, C, C, TAPS)[..., list(TAP_ORDER)]
    arrays = {
        "x": np.ascontiguousarray(x),
        "w_t": np.ascontiguousarray(w.transpose(2, 0, 3, 1).reshape(C, K, TAPS * C)),
        "small": np.ascontiguousarray(np.concatenate([
            np.tile(np.asarray(L0_conv_fc1_w).T, (2, 1)),
            np.tile(np.asarray(L0_conv_bias).T, (2, 1)),
            np.tile(np.asarray(L0_conv_fc1_b)[None], (P, 1)),
            np.tile(np.asarray(L0_conv_fc2_w).reshape(1, K * K), (P, 1)),
            np.tile(np.asarray(L0_conv_fc2_b)[None], (P, 1)),
        ], axis=1)),
    }
    nc = bacc.Bacc("TRN2", target_bir_lowering=False, num_devices=1)
    ins = [nc.dram_tensor(n, a.shape, mybir.dt.from_np(a.dtype), kind="ExternalInput").ap()
           for n, a in arrays.items()]
    out = nc.dram_tensor("out", (B, C, H, W), mybir.dt.float32, kind="ExternalOutput").ap()
    dynamic_conv(nc, *ins, out)
    r = run_bass_kernel_spmd(nc, [arrays], core_ids=[0])
    return r.results[0]["out"]
```
